# Optimizing a Trainium2 kernel written in Bass

```python
import numpy as np
import jax
import jax.numpy as jnp

def _softmax(x, axis=-1):
    return jax.nn.softmax(x, axis=axis)

def _gelu(x):
    return jax.nn.gelu(x, approximate=True)

def _silu(x):
    return jax.nn.silu(x)

def _sigmoid(x):
    return jax.nn.sigmoid(x)

def _layernorm(x, axis=-1, eps=1e-05):
    m = jnp.mean(x, axis=axis, keepdims=True)
    v = jnp.var(x, axis=axis, keepdims=True)
    return (x - m) / jnp.sqrt(v + eps)

def _scatter_add(tgt, idx, src, axis=0):
    return tgt.at[idx].add(src)

def _segment_sum(src, seg, n):
    return jax.ops.segment_sum(src, seg, n)
kernel_name = 'mk_recurrent_d1_jaxref_r8_4ffe1e'

def setup_inputs(seed: int=0):
    np.random.seed(seed)
    _w = jnp.asarray

    def _L0_attn_setup():
        import jax, jax.numpy as jnp
        import numpy as np
        B, S, HID = (1, 256, 512)
        H, NOPE, ROPE, VD = (32, 128, 64, 128)
        QKD = NOPE + ROPE
        Q_RANK, KV_RANK = (192, 64)
        IDX_H, IDX_D, TOPK = (16, 128, 128)
        EPS, THETA = (1e-05, 10000.0)

        def rmsnorm(x, w):
            return x * jax.lax.rsqrt(jnp.mean(x * x, axis=-1, keepdims=True) + EPS) * w

        def rope_interleaved(x, pos):
            d = x.shape[-1]
            inv_freq = 1.0 / THETA ** (jnp.arange(0, d, 2, dtype=jnp.float32) / d)
            ang = pos[:, None] * inv_freq[None, :]
            cos, sin = (jnp.cos(ang), jnp.sin(ang))
            x2 = x.reshape(*x.shape[:-1], d // 2, 2)
            x0, x1 = (x2[..., 0], x2[..., 1])
            return jnp.stack([x0 * cos - x1 * sin, x1 * cos + x0 * sin], axis=-1).reshape(x.shape)
        key = jax.random.key(seed)
        ks = jax.random.split(key, 12)
        s = 0.02
        return {'hidden_states': jax.random.normal(ks[0], (B, S, HID), jnp.float32), 'q_a_w': jax.random.normal(ks[1], (HID, Q_RANK), jnp.float32) * s, 'q_a_norm_w': jnp.ones((Q_RANK,), jnp.float32), 'q_b_w': jax.random.normal(ks[2], (Q_RANK, H * QKD), jnp.float32) * s, 'kv_a_w': jax.random.normal(ks[3], (HID, KV_RANK + ROPE), jnp.float32) * s, 'kv_a_norm_w': jnp.ones((KV_RANK,), jnp.float32), 'kv_b_w': jax.random.normal(ks[4], (KV_RANK, H * (NOPE + VD)), jnp.float32) * s, 'o_w': jax.random.normal(ks[5], (H * VD, HID), jnp.float32) * s, 'idx_wq_w': jax.random.normal(ks[6], (HID, IDX_H * IDX_D), jnp.float32) * s, 'idx_wk_w': jax.random.normal(ks[7], (HID, IDX_D), jnp.float32) * s, 'idx_weights_w': jax.random.normal(ks[8], (HID, IDX_H), jnp.float32) * s}
    _L0_attn_in = _L0_attn_setup()

    def _L0_ffn_setup():
        import jax, jax.numpy as jnp
        import numpy as np
        B, S, D, O, E, R = (2, 512, 512, 512, 8, 16)
        TOP_K = 2
        SCALING = 32.0 / 16.0
        key = jax.random.key(seed)
        k = jax.random.split(key, 6)
        x = jax.random.normal(k[0], (B, S, D), dtype=jnp.float32)
        W_base = jax.random.normal(k[1], (O, D), dtype=jnp.float32) * 0.02
        b_base = jax.random.normal(k[2], (O,), dtype=jnp.float32) * 0.02
        W_router = jax.random.normal(k[3], (E, D), dtype=jnp.float32) * 0.01
        lora_A = jax.random.normal(k[4], (E, R, D), dtype=jnp.float32) * (1.0 / np.sqrt(D))
        lora_B = jax.random.normal(k[5], (E, O, R), dtype=jnp.float32) * 0.02
        return {'x': x, 'W_base': W_base, 'b_base': b_base, 'W_router': W_router, 'lora_A': lora_A, 'lora_B': lora_B}
    _L0_ffn_in = _L0_ffn_setup()
    _d = {'L0_attn_hidden_states': _L0_attn_in['hidden_states'], 'L0_attn_q_a_w': _L0_attn_in['q_a_w'], 'L0_attn_q_a_norm_w': _L0_attn_in['q_a_norm_w'], 'L0_attn_q_b_w': _L0_attn_in['q_b_w'], 'L0_attn_kv_a_w': _L0_attn_in['kv_a_w'], 'L0_attn_kv_a_norm_w': _L0_attn_in['kv_a_norm_w'], 'L0_attn_kv_b_w': _L0_attn_in['kv_b_w'], 'L0_attn_o_w': _L0_attn_in['o_w'], 'L0_attn_idx_wq_w': _L0_attn_in['idx_wq_w'], 'L0_attn_idx_wk_w': _L0_attn_in['idx_wk_w'], 'L0_attn_idx_weights_w': _L0_attn_in['idx_weights_w'], 'L0_ffn_W_base': _L0_ffn_in['W_base'], 'L0_ffn_b_base': _L0_ffn_in['b_base'], 'L0_ffn_W_router': _L0_ffn_in['W_router'], 'L0_ffn_lora_A': _L0_ffn_in['lora_A'], 'L0_ffn_lora_B': _L0_ffn_in['lora_B']}
    _x0 = _d['L0_attn_hidden_states']
    _d['L0_attn_hidden_states'] = jax.random.normal(jax.random.fold_in(jax.random.key(seed), 1), (1, 1024, 512), dtype=_x0.dtype)
    del _x0
    return _d

def reference(L0_attn_hidden_states, L0_attn_q_a_w, L0_attn_q_a_norm_w, L0_attn_q_b_w, L0_attn_kv_a_w, L0_attn_kv_a_norm_w, L0_attn_kv_b_w, L0_attn_o_w, L0_attn_idx_wq_w, L0_attn_idx_wk_w, L0_attn_idx_weights_w, L0_ffn_W_base, L0_ffn_b_base, L0_ffn_W_router, L0_ffn_lora_A, L0_ffn_lora_B):

    def _L0_attn_ref(hidden_states, q_a_w, q_a_norm_w, q_b_w, kv_a_w, kv_a_norm_w, kv_b_w, o_w, idx_wq_w, idx_wk_w, idx_weights_w):
        import jax, jax.numpy as jnp
        import numpy as np
        B, S, HID = (1, 256, 512)
        H, NOPE, ROPE, VD = (32, 128, 64, 128)
        QKD = NOPE + ROPE
        Q_RANK, KV_RANK = (192, 64)
        IDX_H, IDX_D, TOPK = (16, 128, 128)
        EPS, THETA = (1e-05, 10000.0)

        def rmsnorm(x, w):
            return x * jax.lax.rsqrt(jnp.mean(x * x, axis=-1, keepdims=True) + EPS) * w

        def rope_interleaved(x, pos):
            d = x.shape[-1]
            inv_freq = 1.0 / THETA ** (jnp.arange(0, d, 2, dtype=jnp.float32) / d)
            ang = pos[:, None] * inv_freq[None, :]
            cos, sin = (jnp.cos(ang), jnp.sin(ang))
            x2 = x.reshape(*x.shape[:-1], d // 2, 2)
            x0, x1 = (x2[..., 0], x2[..., 1])
            return jnp.stack([x0 * cos - x1 * sin, x1 * cos + x0 * sin], axis=-1).reshape(x.shape)
        b, s, _ = hidden_states.shape
        pos = jnp.arange(s, dtype=jnp.float32)
        q_lat = rmsnorm(hidden_states @ q_a_w, q_a_norm_w)
        q = (q_lat @ q_b_w).reshape(b, s, H, QKD).transpose(0, 2, 1, 3)
        q_nope, q_pe = (q[..., :NOPE], q[..., NOPE:])
        ckv = hidden_states @ kv_a_w
        kv_lat, k_pe = (ckv[..., :KV_RANK], ckv[..., KV_RANK:])
        kv = (rmsnorm(kv_lat, kv_a_norm_w) @ kv_b_w).reshape(b, s, H, NOPE + VD).transpose(0, 2, 1, 3)
        k_nope, v = (kv[..., :NOPE], kv[..., NOPE:])
        q_pe = rope_interleaved(q_pe, pos)
        k_pe = rope_interleaved(k_pe[:, None, :, :], pos)
        scores = (jnp.einsum('bhqd,bhkd->bhqk', q_nope, k_nope) + jnp.einsum('bhqd,bhkd->bhqk', q_pe, k_pe)) * QKD ** (-0.5)
        iq = (hidden_states @ idx_wq_w).reshape(b, s, IDX_H, IDX_D)
        ik = hidden_states @ idx_wk_w
        iw = hidden_states @ idx_weights_w * IDX_H ** (-0.5)
        idx_scores = jnp.einsum('bqn,bnqk->bqk', iw, jax.nn.relu(jnp.einsum('bqnd,bkd->bnqk', iq, ik))) * IDX_D ** (-0.5)
        causal = pos[:, None] >= pos[None, :]
        idx_scores = jnp.where(causal, idx_scores, -jnp.inf)
        _, topk_idx = jax.lax.top_k(idx_scores, TOPK)
        bi = jnp.arange(b)[:, None, None]
        qi = jnp.arange(s)[None, :, None]
        topk_mask = jnp.zeros((b, s, s), bool).at[bi, qi, topk_idx].set(True)
        mask = topk_mask & causal
        scores = jnp.where(mask[:, None], scores, -jnp.inf)
        attn = jax.nn.softmax(scores, axis=-1)
        out = jnp.einsum('bhqk,bhkd->bqhd', attn, v).reshape(b, s, H * VD)
        return out @ o_w

    def _L0_ffn_ref(x, W_base, b_base, W_router, lora_A, lora_B):
        import jax, jax.numpy as jnp
        import numpy as np
        B, S, D, O, E, R = (2, 512, 512, 512, 8, 16)
        TOP_K = 2
        SCALING = 32.0 / 16.0
        d = x.shape[-1]
        n_experts = W_router.shape[0]
        xf = x.reshape(-1, d)
        logits = xf @ W_router.T
        probs = jax.nn.softmax(logits, axis=-1)
        topk_p, topk_i = jax.lax.top_k(probs, TOP_K)
        topk_p = topk_p / jnp.sum(topk_p, axis=-1, keepdims=True)
        w = jnp.sum(jax.nn.one_hot(topk_i, n_experts, dtype=xf.dtype) * topk_p[..., None], axis=1)
        h = jnp.einsum('td,erd->ter', xf, lora_A)
        lora_out = jnp.einsum('ter,eor,te->to', h, lora_B, w) * SCALING
        base = x @ W_base.T + b_base
        return base + lora_out.reshape(x.shape[:-1] + (W_base.shape[0],))
    x = L0_attn_hidden_states
    xn = _layernorm(x, axis=-1)
    s = _L0_attn_ref(xn, L0_attn_q_a_w, L0_attn_q_a_norm_w, L0_attn_q_b_w, L0_attn_kv_a_w, L0_attn_kv_a_norm_w, L0_attn_kv_b_w, L0_attn_o_w, L0_attn_idx_wq_w, L0_attn_idx_wk_w, L0_attn_idx_weights_w)
    g = _silu(_L0_ffn_ref(xn, L0_ffn_W_base, L0_ffn_b_base, L0_ffn_W_router, L0_ffn_lora_A, L0_ffn_lora_B))
    x = x + s * g
    return x

_drawn_inputs = setup_inputs


def setup_inputs(seed=0):
    import zlib

    import numpy as np

    out = dict(_drawn_inputs(seed))
    spreads = {'L0_attn_q_a_norm_w': (1.0, 0.6), 'L0_attn_kv_a_norm_w': (1.0, 0.6)}
    factors = {'L0_attn_q_a_w': 8.0,
     'L0_attn_q_b_w': 8.0,
     'L0_attn_kv_a_w': 5.585,
     'L0_attn_kv_b_w': 5.64,
     'L0_attn_o_w': 4.845,
     'L0_attn_idx_wq_w': 8.0,
     'L0_attn_idx_wk_w': 8.0,
     'L0_attn_idx_weights_w': 8.0,
     'L0_ffn_W_base': 6.577,
     'L0_ffn_b_base': 25.552,
     'L0_ffn_W_router': 8.0,
     'L0_ffn_lora_A': 8.0,
     'L0_ffn_lora_B': 8.0}
    for name, (base, spread) in spreads.items():
        noise = np.random.default_rng([zlib.crc32(name.encode()), seed]).standard_normal(out[name].shape)
        drawn = base * np.exp(spread * noise) if base else spread * noise
        out[name] = jnp.asarray(drawn.astype(out[name].dtype))
    for name, factor in factors.items():
        out[name] = (out[name] * factor).astype(out[name].dtype)
    return out
```

```python
from contextlib import ExitStack

import concourse.bass as bass
from concourse import mybir

F32 = mybir.dt.float32
F16 = mybir.dt.float16
BF16 = mybir.dt.bfloat16
U32 = mybir.dt.uint32
ALU = mybir.AluOpType
ACT = mybir.ActivationFunctionType
AX = mybir.AxisListType.X

P = 128
S, HID = 1024, 512
NT = S // P
GT = 4
GW = GT * P
NG = NT // GT
HC = HID // P
H, NOPE, ROPE, VD = 32, 128, 64, 128
QR, KVR = 192, 64
NP = H // 2
IH, ID, TOPK = 16, 128, 128
E, R = 8, 16
EPS = 1e-5
CQ, CKV, CPE, CIW, CRT, CLO = 0, QR, QR + KVR, QR + KVR + ROPE, QR + KVR + ROPE + IH, QR + KVR + ROPE + IH + E
NPROJ = CLO + E * R
SCALE = float(NOPE + ROPE) ** -0.5
IW_SCALE = float(IH) ** -0.5 * float(ID) ** -0.5
LORA_SCALE = 2.0
FUTURE = -3.0e38
TAKEN = -3.4e38
BAR = -3.2e38
MASKED = -1.0e30
ROUNDS = TOPK // 8
LAG = 2
NBUF = 4


def extent(t):
    return (t + 1) * P


def acc_at(t):
    return sum(extent(k) for k in range(1, t))


def mask_at(t):
    return sum(extent(k) for k in range(t))


def splits(t):
    n = t + 1
    if n <= 4:
        return [(0, n)]
    return [(0, (n + 1) // 2), ((n + 1) // 2, n // 2)]


def plan(g):
    out = []
    for j in range(2 * GT):
        t = GT * g + j % GT
        parts = splits(t)
        for n, (b0, nb) in enumerate(parts):
            out.append((j, j // GT, j % GT, t, b0, nb, n == len(parts) - 1))
    return out


def uses(g):
    chunks = plan(g)
    out = []
    for j in range(2 * GT):
        if j == 0:
            out.append(("c", 0, j))
        if j == 1:
            out.append(("pe", 0, j))
        if j == 2:
            out.append(("sw", 0, j))
        if j == 4:
            out.append(("o", 0, j))
        for c, ch in enumerate(chunks):
            if ch[0] == j:
                out.append(("chunk", c, j))
    return out


def transposed(g, p, j):
    chunks = plan(g)
    q = p if j >= 0 else p - 1
    return q * len(chunks) + (1 + max(c for c, ch in enumerate(chunks) if ch[0] == j % 8))


def build(nc, A):
    with ExitStack() as ctx:
        def sb(name, shape, dt=F32):
            return ctx.enter_context(nc.sbuf_tensor(name, shape, dt))

        def psum(name, shape):
            return ctx.enter_context(nc.psum_tensor(name, shape, F32))

        def sem(name):
            return ctx.enter_context(nc.semaphore(name))

        psS = psum("psS", [P, 2, 1024])
        psT = psum("psT", [P, 2, 512])
        psO = psum("psO", [P, 2, 512])

        OT = sb("OT", [P, NP * S])
        OTv = OT[:, :].rearrange("p (n s) -> p n s", n=NP)
        Wvo = sb("Wvo", [P, NP * HID])
        Wc1 = sb("Wc1", [P, NP * P])
        low = sb("low", [P, NP * P])
        Wc2 = low[0:QR - P, :]
        qT2 = low[QR - P:P, 0:S]
        stage2 = low[QR - P:P, S:S + 3 * P].rearrange("p (a n) -> p a n", a=3)
        KT = sb("KT", [P, S])
        KF = sb("KF", [P, S])
        ikT = sb("ikT", [P, S])
        qT1 = sb("qT1", [P, S])
        acc = sb("acc", [P, acc_at(NT)])
        maskb = sb("maskb", [P, mask_at(NT)], BF16)
        Vhl = sb("Vhl", [P, NT, 2, KVR], F16)
        iw = sb("iw", [P, NT, IH])
        ropeC = sb("ropeC", [P, S])
        ropeS = sb("ropeS", [P, S])
        ident = sb("ident", [P, P])
        stage1 = sb("stage1", [P, 3, P])
        wslot = sb("wslot", [P, 2, HC, P])
        Sm = sb("Sm", [P, 2, S])
        Pr = sb("Pr", [P, 2, S])
        PTh = sb("PTh", [P, NBUF, 512], F16)
        PTl = sb("PTl", [P, NBUF, 512], F16)
        qAB = sb("qAB", [P, 2, GW])
        cT = ikT[:, 0:GW]
        m1 = ikT[:, GW:2 * GW]
        m2 = sb("m2", [P, GW])
        nmax = sb("nmax", [P, 2 * GT])
        den = sb("den", [P, 2 * GT])
        rden = sb("rden", [P, 2 * GT])
        osum = sb("osum", [P, 2, GT, KVR])
        On = sb("On", [P, GT, 2, KVR])
        top8 = sb("top8", [P, GT, 8])
        small = sb("small", [P, 320])
        wkv2 = sb("wkv2", [P, 1])

        def early(lo, n):
            return OT[:, lo:lo + n]

        at = 0
        xin = early(at, NT * HID).rearrange("p (t d) -> p t d", t=NT); at += NT * HID
        pj = early(at, NT * NPROJ).rearrange("p (t n) -> p t n", t=NT); at += NT * NPROJ
        xnT = early(at, HC * S).rearrange("p (c s) -> p c s", c=HC); at += HC * S
        wproj = early(at, HC * NPROJ).rearrange("p (c n) -> p c n", c=HC); at += HC * NPROJ
        ktab = early(at, NT * ROPE).rearrange("p (t a n) -> p t a n", t=NT, a=2); at += NT * ROPE
        loraB = early(at, HID); at += HID
        bias = early(at, HID); at += HID
        wqb = early(at, QR); at += QR
        wkvb = early(at, KVR); at += KVR
        assert at <= NP * S
        WbT = Wc1[:, :].rearrange("p (c n) -> p c n", c=HC)
        hwT = Pr[:, 0, :]
        hw = Sm[:, 0, :].rearrange("p (t e r) -> p t e r", t=NT, e=E)
        kbuf = Wvo[:, 0:NT * 192].rearrange("p (t n) -> p t n", t=NT)
        qn = Wvo[:, NT * 192:NT * 384].rearrange("p (t n) -> p t n", t=NT)
        latn = Wvo[:, NT * 384:NT * 448].rearrange("p (t n) -> p t n", t=NT)
        tmp = Wvo[:, NT * 448:NT * (448 + 192)].rearrange("p (t n) -> p t n", t=NT)
        gate = xin

        g_dram = nc.dram_tensor("g_scratch", [NT, P, HID], F32, kind="Internal").ap()

        def sems(names):
            return [sem(n) for n in names.split()]

        (s_w, s_w2, s_ident, s_mv, s_sd, s_xn, s_xt, s_xc, s_pj, s_pjc, s_ik, s_ikc, s_kq, s_kt, s_ktc,
         s_vec, s_act, s_rexp, s_sq, s_hw, s_hwt, s_hwc, s_bt, s_y, s_ey, s_g, s_gd, s_accz,
         s_wd0, s_wd1, s_wm, s_wcc, s_wbfree, s_init, s_passed) = sems(
            "s_w s_w2 s_ident s_mv s_sd s_xn s_xt s_xc s_pj s_pjc s_ik s_ikc s_kq s_kt s_ktc "
            "s_vec s_act s_rexp s_sq s_hw s_hwt s_hwc s_bt s_y s_ey s_g s_gd s_accz "
            "s_wd0 s_wd1 s_wm s_wcc s_wbfree s_init s_passed")
        chain = {"n": 0}

        block = ctx.enter_context(nc.Block())

        def W(eng, s, v):
            if isinstance(v, int) and v <= 0:
                return
            eng.wait_ge(s, v)

        def own(eng):
            eng.sem_inc(s_passed, 1)

        s_x = [sem(f"s_x{t}") for t in range(NT)]
        IX = [dict(zip("dma0 dma1 q qc sc relu acc top mask wfree".split(),
                       sems(" ".join(f"ix{g}_{n}" for n in "dma0 dma1 q qc sc relu acc top mask wfree".split()))))
              for g in range(NG)]
        AT = [dict(zip("dma qp qa qb sc masked exp pt cps m12 hi lo on onrm otr ot ln".split(),
                       sems(" ".join(f"at{g}_{n}" for n in
                                     "dma qp qa qb sc masked exp pt cps m12 hi lo on onrm otr ot ln".split()))))
              for g in range(NG)]
        s_fin, s_fd0, s_fd1, s_fy, s_fo0, s_fo1, s_fadd, s_ffree = sems("s_fin s_fd0 s_fd1 s_fy s_fo0 s_fo1 s_fadd s_ffree")

        def load_head(sp, slot, h):
            dst = wslot[:, slot, :, :].rearrange("p c n -> p (c n)")
            sp.dma_start(dst[:, 0:320], A["headw"][bass.ds(h, 1)].rearrange("a p n -> p (a n)")).then_inc((s_wd0, s_wd1)[slot], 16)
            sp.dma_start(qAB[:, slot, :], A["o_w"][bass.ds(h * VD, VD), :]).then_inc((s_wd0, s_wd1)[slot], 16)

        def load_index(sp, s, slot, n):
            sp.dma_start(wslot[:, slot, :, :],
                         A["iq_w"].rearrange("(c p) n -> p c n", p=P)[:, :, bass.ds(n * ID, ID)]).then_inc(s[f"dma{slot}"], 16)

        def load_pair(sp, s, p):
            sp.dma_start(stage1[:, 1:3, :], A["pairw"][bass.ds(p, 1), 0:P].rearrange("a r b n -> r (a b) n")).then_inc(s["dma"], 16)
            sp.dma_start(stage2[:, 1:3, :], A["pairw"][bass.ds(p, 1), P:QR].rearrange("a r b n -> r (a b) n")).then_inc(s["dma"], 16)
            sp.dma_start(stage1[:, 0, :], Wc1[:, bass.ds(p * P, P)]).then_inc(s["dma"], 16)
            sp.dma_start(stage2[:, 0, :], Wc2[:, bass.ds(p * P, P)]).then_inc(s["dma"], 16)

        @block.sync
        def _(sp):
            for t in range(NT):
                sp.dma_start(xin[:, t, :], A["x"][t * P:(t + 1) * P, :]).then_inc(s_x[t], 16)
                if t == 0:
                    sp.dma_start(wproj, A["wproj"].rearrange("(c p) n -> p c n", p=P)).then_inc(s_w, 16)
            sp.dma_start(wslot[:, 0, :, :], A["ik_w"].rearrange("(c p) n -> p c n", p=P)).then_inc(s_w2, 16)
            for dst, src in ((wqb, A["wq_norm"].partition_broadcast(P)), (wkvb, A["wkv_norm"].partition_broadcast(P)),
                             (ktab, A["ktab"].rearrange("(t p) a n -> p t a n", p=P)),
                             (wkv2[0:KVR, :], A["wkv_norm"].rearrange("(n a) -> n a", a=1)),
                             (wkv2[KVR:P, :], A["wkv_norm"].rearrange("(n a) -> n a", a=1)),
                             (bias, A["b_base"].partition_broadcast(P)),
                             (loraB, A["lora_B"]),
                             (WbT, A["WbT"].rearrange("(c p) n -> p c n", p=P)),
                             (ropeC[:, :], A["ropeC"]), (ropeS[:, :], A["ropeS"])):
                sp.dma_start(dst, src).then_inc(s_w2, 16)
            for t in range(NT):
                sp.wait_ge(s_g, t + 1)
                sp.dma_start(g_dram[t], gate[:, t, :]).then_inc(s_gd, 16)
            sp.wait_ge(s_ikc, 2)
            for slot in range(2):
                load_head(sp, slot, slot)
            with sp.Fori(1, NP) as p:
                for slot in range(2):
                    sp.wait_ge(s_wm, p * 4 + (2 * slot - 2))
                    load_head(sp, slot, p * 2 + slot)
            sp.wait_ge(s_wm, 4 * NP)
            for g in range(NG):
                s = IX[g]
                if g:
                    sp.wait_ge(IX[0]["q"], IH)
                for slot in range(2):
                    load_index(sp, s, slot, slot)
                with sp.Fori(1, IH // 2) as i:
                    for slot in range(2):
                        sp.wait_ge(s["q"], i * 2 + (slot - 1))
                        load_index(sp, s, slot, i * 2 + slot)
            for g in range(NG):
                s = AT[g]
                if g:
                    sp.wait_ge(AT[0]["qp"], 3 * NP)
                else:
                    sp.wait_ge(s_wcc, 2 * H)
                load_pair(sp, s, 0)
                with sp.Fori(1, NP) as p:
                    sp.wait_ge(s["qp"], p * 3)
                    load_pair(sp, s, p)
            sp.wait_ge(s_gd, 16 * NT)
            sp.wait_ge(AT[1]["masked"], NP * 2 * GT)
            sp.wait_ge(AT[1]["exp"], NP * 2 * GT)
            for t in range(NT):
                if t >= 2:
                    sp.wait_ge(s_fadd, t - 1)
                sp.dma_start(Sm[:, t % 2, 0:HID], A["x"][t * P:(t + 1) * P, :]).then_inc((s_fd0, s_fd1)[t % 2], 16)
                sp.dma_start(Sm[:, t % 2, HID:2 * HID], g_dram[t]).then_inc((s_fd0, s_fd1)[t % 2], 16)
                if t >= 1:
                    sp.wait_ge(s_fadd, t)
                    sp.dma_start(A["out"][(t - 1) * P:t * P, :], m1[:, :] if t % 2 else m2[:, :]).then_inc((s_fo0, s_fo1)[(t - 1) % 2], 16)
            sp.wait_ge(s_fadd, NT)
            sp.dma_start(A["out"][(NT - 1) * P:, :], m2[:, :] if (NT - 1) % 2 else m1[:, :]).then_inc((s_fo0, s_fo1)[(NT - 1) % 2], 16)
            sp.wait_ge(s_fo0, 16 * NT // 2)
            sp.wait_ge(s_fo1, 16 * NT // 2)

        @block.gpsimd
        def _(pool):
            nc.gpsimd.memset(ident[:, :], 0.0).then_inc(s_init, 1)
            nc.gpsimd.memset(acc[:, :], 0.0).then_inc(s_init, 1)
            nc.gpsimd.memset(maskb[:, 0:P], 0.0).then_inc(s_init, 1)
            nc.gpsimd.iota(small[:, 312:320].bitcast(mybir.dt.int32), pattern=[[1, E]], base=0, channel_multiplier=0).then_inc(s_init, 1)
            pool.wait_ge(s_init, 4)
            nc.gpsimd.affine_select(out=ident[:, :], in_=ident[:, :], compare_op=ALU.not_equal, fill=1.0,
                                    base=0, pattern=[[-1, P]], channel_multiplier=1).then_inc(s_ident, 1)
            nc.gpsimd.affine_select(out=maskb[:, 0:P], in_=maskb[:, 0:P], compare_op=ALU.is_ge, fill=MASKED,
                                    base=0, pattern=[[-1, P]], channel_multiplier=1).then_inc(s_accz, 1)
            for t in range(1, NT):
                d = acc[:, acc_at(t) + t * P:acc_at(t) + (t + 1) * P]
                nc.gpsimd.affine_select(out=d, in_=d, compare_op=ALU.is_ge, fill=FUTURE,
                                        base=0, pattern=[[-1, P]], channel_multiplier=1).then_inc(s_accz, 1)

            def queries(s, p):
                pool.wait_ge(s["m12"], p * 2 + 2)
                pool.wait_ge(s["cps"], p + 1)
                W(pool, s["sc"], p * 8 - 4)
                own(pool)
                nc.gpsimd.tensor_copy(qAB[0:64, 0, :], cT[0:64, :]).then_inc(s["qa"], 1)
                nc.gpsimd.tensor_tensor(qAB[64:P, 0, :], m1[64:P, :], m2[64:P, :], ALU.add).then_inc(s["qa"], 1)
                W(pool, s["sc"], p * 8)
                own(pool)
                nc.gpsimd.tensor_copy(qAB[64:P, 1, :], cT[64:P, :]).then_inc(s["qb"], 1)
                nc.gpsimd.tensor_tensor(qAB[0:64, 1, :], m1[0:64, :], m2[0:64, :], ALU.add).then_inc(s["qb"], 1)

            pool.wait_ge(IX[1]["sc"], IH * GT)
            for g in range(NG):
                s = AT[g]
                if g:
                    pool.wait_ge(AT[0]["sc"], NP * 2 * GT)
                queries(s, 0)
                with pool.Fori(1, NP) as p:
                    queries(s, p)

        @block.scalar
        def _(act):
            na = [0]

            def link(ins):
                na[0] += 1
                ins.then_inc(s_act, 1)
                act.wait_ge(s_act, na[0])

            act.wait_ge(s_mv, 1)
            nc.scalar.activation(small[:, 24:32], small[:, 16:24], ACT.Sqrt).then_inc(s_sd, 1)
            for t in range(NT):
                act.wait_ge(s_xt, t + 1)
                nc.scalar.activation(xnT[:, :, t * P:(t + 1) * P], psT[:, t % 2, :].rearrange("p (c n) -> p c n", c=HC),
                                     ACT.Copy).then_inc(s_xc, 1)
                act.wait_ge(s_pj, t + 1)
                nc.scalar.activation(pj[:, t, :], psO[:, t % 2, 0:NPROJ], ACT.Copy).then_inc(s_pjc, 1)
            act.wait_ge(s_sq, 1)
            nc.scalar.activation(small[:, 64:80], small[:, 48:64], ACT.Sqrt).then_inc(s_sd, 1)
            for k in range(2):
                act.wait_ge(s_ik, k + 1)
                nc.scalar.activation(ikT[:, k * 512:(k + 1) * 512], psS[:, 0, k * 512:(k + 1) * 512], ACT.Copy).then_inc(s_ikc, 1)
            act.wait_ge(s_rexp, 1)
            nc.scalar.activation(small[:, 88:152], small[:, 88:152], ACT.Exp).then_inc(s_rexp, 1)
            for t in range(NT):
                act.wait_ge(s_kt, t + 1)
                c = slice(t * P, (t + 1) * P)
                nc.scalar.activation(KT[:, c], psT[:, t % 2, 0:P], ACT.Copy).then_inc(s_ktc, 1)
                nc.scalar.activation(KF[:, c], psT[:, t % 2, P:2 * P], ACT.Copy).then_inc(s_ktc, 1)
                nc.scalar.activation(qT1[:, c], psT[:, t % 2, 2 * P:3 * P], ACT.Copy).then_inc(s_ktc, 1)
                nc.scalar.activation(qT2[:, c], psT[0:QR - P, t % 2, 3 * P:4 * P], ACT.Copy).then_inc(s_ktc, 1)
            for t in range(NT):
                act.wait_ge(s_hwt, t + 1)
                nc.scalar.activation(hwT[:, t * P:(t + 1) * P], psO[:, t % 2, 0:P], ACT.Copy).then_inc(s_hwc, 1)
            for t in range(NT):
                act.wait_ge(s_y, t + 1)
                nc.scalar.activation(Pr[:, 1, (t % 2) * HID:(t % 2) * HID + HID], gate[:, t, :], ACT.Exp, scale=-1.0).then_inc(s_ey, 1)
            with act.Fori(0, NP) as p:
                for k in range(2):
                    act.wait_ge(s_wm, p * 4 + (2 * k + 1))
                    nc.scalar.activation(Wc1[:, bass.ds(p * P + k * 64, 64)], psT[:, k, 0:64], ACT.Copy).then_inc(s_wcc, 1)
                    nc.scalar.activation(Wc2[:, bass.ds(p * P + k * 64, 64)], psT[0:QR - P, k, 64:128], ACT.Copy).then_inc(s_wcc, 1)
            for g in range(NG):
                s = IX[g]
                tiles = [t for t in range(GT * g, GT * g + GT) if t]
                n = len(tiles)

                def head(i, slot, first):
                    act.wait_ge(s["q"], i * 2 + (slot + 1))
                    if not first:
                        act.wait_ge(s["sc"], i * (2 * n) + (slot * n - n))
                    nc.scalar.activation(qAB[:, slot, :], psT[:, slot, :], ACT.Copy).then_inc(s["qc"], 1)
                    for k, t in enumerate(tiles):
                        idx = i * (2 * n) + (slot * n + k)
                        act.wait_ge(s["sc"], idx + 1)
                        if not (first and slot * n + k < 2):
                            act.wait_ge(s["acc"], idx - 1)
                        b = (slot * n + k) % 2
                        nc.scalar.activation(Sm[:, b, 0:extent(t)], psS[:, b, 0:extent(t)], ACT.Relu).then_inc(s["relu"], 1)

                if g:
                    act.wait_ge(IX[0]["acc"], IH * (GT - 1))
                head(0, 0, True)
                head(0, 1, True)
                with act.Fori(1, IH // 2) as i:
                    head(i, 0, False)
                    head(i, 1, False)
            for g in range(NG):
                s = AT[g]
                seq = uses(g)
                chunks = plan(g)
                nch = len(chunks)

                def exp(p, j, first, last_of_prev=False):
                    act.wait_ge(s["masked"], p * 8 + (j + 1))
                    if not (first and j < 2):
                        act.wait_ge(s["pt"], transposed(g, p, j - 2))
                    if not first and j % GT == 0:
                        act.wait_ge(s["onrm"], p * 2 + (j // GT - 1))
                    t = GT * g + j % GT
                    nc.scalar.activation(Pr[:, j % 2, 0:extent(t)], Sm[:, j % 2, 0:extent(t)], ACT.Exp,
                                         bias=nmax[:, j:j + 1], scale=-1.0, accum_out=den[:, j:j + 1]).then_inc(s["exp"], 1)

                def body(p, first, last):
                    for u, (kind, c, j) in enumerate(seq):
                        bank = u % 2
                        if kind == "chunk" and (c == 0 or chunks[c - 1][0] != j):
                            if j < 7:
                                exp(p, j + 1, first)
                            elif not last:
                                exp(p + 1, 0, False)
                        if kind == "c" and not last:
                            act.wait_ge(s["qp"], p * 3 + 4)
                            act.wait_ge(s["qb"], p * 2 + 2)
                            nc.scalar.activation(cT[:, :], psT[:, bank, :], ACT.Copy).then_inc(s["cps"], 1)
                        elif kind == "o" and not first:
                            act.wait_ge(s["otr"], p)
                            nc.scalar.activation(OT[:, bass.ds((p - 1) * S + g * GW, GW)], psT[:, bank, :],
                                                 ACT.Copy).then_inc(s["ot"], 1)
                        elif kind == "chunk":
                            nb = chunks[c][5]
                            act.wait_ge(s["pt"], p * nch + (c + 1))
                            if not (first and c < NBUF):
                                act.wait_ge(s["on"], p * nch + (c - NBUF + 1))
                            nc.scalar.activation(PTh[:, c % NBUF, 0:nb * P], psT[:, bank, 0:nb * P], ACT.Copy).then_inc(s["hi"], 1)

                if g:
                    act.wait_ge(AT[0]["onrm"], 2 * NP)
                else:
                    act.wait_ge(s_gd, 16 * NT)
                act.wait_ge(s["qp"], 1)
                nc.scalar.activation(cT[:, :], psT[:, 0, :], ACT.Copy).then_inc(s["cps"], 1)
                exp(0, 0, True)
                body(0, True, False)
                with act.Fori(1, NP - 1) as p:
                    body(p, False, False)
                body(NP - 1, False, True)
                act.wait_ge(s["otr"], NP)
                nc.scalar.activation(OT[:, (NP - 1) * S + g * GW:(NP - 1) * S + (g + 1) * GW], psT[:, 0, :], ACT.Copy).then_inc(s["ot"], 1)

        def finish_gate(dve, link, t):
            e = Pr[:, 1, (t % 2) * HID:(t % 2) * HID + HID]
            dve.wait_ge(s_ey, t + 1)
            link(nc.vector.tensor_scalar(e, e, 1.0, None, ALU.add))
            link(nc.vector.reciprocal(e, e))
            nc.vector.tensor_tensor(gate[:, t, :], gate[:, t, :], e, ALU.mult).then_inc(s_g, 1)

        @block.vector
        def _(dve):
            nv = [0]
            V = nc.vector

            def link(ins):
                nv[0] += 1
                ins.then_inc(s_vec, 1)
                dve.wait_ge(s_vec, nv[0])

            def rsqrt_refine(out, x, y, t1):
                link(V.reciprocal(t1, y))
                link(V.tensor_tensor(out, t1, t1, ALU.mult))
                link(V.tensor_tensor(out, out, x, ALU.mult))
                link(V.tensor_scalar(out, out, -0.5, 1.5, ALU.mult, ALU.add))
                link(V.tensor_tensor(out, out, t1, ALU.mult))

            for t in range(NT):
                dve.wait_ge(s_x[t], 16)
                link(V.bn_stats(small[:, 160 + 6 * t:166 + 6 * t], xin[:, t, :]))
                link(V.bn_aggr(small[:, 2 * t:2 * t + 2], small[:, 160 + 6 * t:166 + 6 * t]))
            mv = small[:, 0:16].rearrange("p (t a) -> p t a", a=2)
            V.tensor_scalar(small[:, 16:24], mv[:, :, 1], EPS, None, ALU.add).then_inc(s_mv, 1)
            dve.wait_ge(s_sd, 1)
            dve.wait_ge(s_mv, 1)
            rsqrt_refine(small[:, 32:40], small[:, 16:24], small[:, 24:32], small[:, 40:48])
            for t in range(NT):
                V.tensor_scalar(xin[:, t, :], xin[:, t, :], small[:, 2 * t:2 * t + 1], small[:, 32 + t:33 + t],
                                ALU.subtract, ALU.mult).then_inc(s_xn, 1)
            dve.wait_ge(s_pjc, NT)
            dve.wait_ge(s_w2, 16 * 11)
            link(V.tensor_tensor(tmp, pj[:, :, 0:QR], pj[:, :, 0:QR], ALU.mult))
            link(V.tensor_reduce(small[:, 48:56], tmp, AX, ALU.add))
            link(V.tensor_tensor(tmp[:, :, 0:KVR], pj[:, :, CKV:CKV + KVR], pj[:, :, CKV:CKV + KVR], ALU.mult))
            link(V.tensor_reduce(small[:, 56:64], tmp[:, :, 0:KVR], AX, ALU.add))
            link(V.tensor_scalar(small[:, 48:56], small[:, 48:56], 1.0 / QR, EPS, ALU.mult, ALU.add))
            V.tensor_scalar(small[:, 56:64], small[:, 56:64], 1.0 / KVR, EPS, ALU.mult, ALU.add).then_inc(s_sq, 1)
            lg = pj[:, :, CRT:CRT + E]
            ex = small[:, 88:152].rearrange("p (t e) -> p t e", t=NT)
            link(V.tensor_reduce(small[:, 80:88], lg, AX, ALU.max))
            V.tensor_tensor(ex, lg, small[:, 80:88].unsqueeze(2).broadcast_to([P, NT, E]), ALU.subtract).then_inc(s_rexp, 1)
            dve.wait_ge(s_sd, 2)
            dve.wait_ge(s_sq, 1)
            rsqrt_refine(small[:, 64:80], small[:, 48:64], small[:, 64:80], small[:, 288:304])
            rq, rk = small[:, 64:72], small[:, 72:80]
            link(V.tensor_tensor(qn, pj[:, :, 0:QR], rq.unsqueeze(2).broadcast_to([P, NT, QR]), ALU.mult))
            V.tensor_tensor(qn, qn, wqb.unsqueeze(1).broadcast_to([P, NT, QR]), ALU.mult).then_inc(s_kq, 1)
            link(V.tensor_tensor(latn, pj[:, :, CKV:CKV + KVR], rk.unsqueeze(2).broadcast_to([P, NT, KVR]), ALU.mult))
            wk3 = wkvb.unsqueeze(1).broadcast_to([P, NT, KVR])
            link(V.tensor_tensor(kbuf[:, :, 0:KVR], latn, wk3, ALU.mult))
            link(V.tensor_tensor(kbuf[:, :, 128:192], latn, wk3, ALU.mult))
            link(V.tensor_copy(Vhl[:, :, 0, :], latn))
            link(V.tensor_tensor(Vhl[:, :, 1, :], latn, Vhl[:, :, 0, :], ALU.subtract))
            pe = pj[:, :, CPE:CPE + ROPE].rearrange("p t (i a) -> p t i a", a=2)
            ro = kbuf[:, :, KVR:KVR + ROPE].rearrange("p t (i a) -> p t i a", a=2)
            tr4 = tmp[:, :, 0:ROPE].rearrange("p t (i a) -> p t i a", a=2)
            cos, sin = ktab[:, :, 0, :], ktab[:, :, 1, :]
            link(V.tensor_tensor(ro[:, :, :, 0], pe[:, :, :, 0], cos, ALU.mult))
            link(V.tensor_tensor(ro[:, :, :, 1], pe[:, :, :, 1], cos, ALU.mult))
            link(V.tensor_tensor(tr4[:, :, :, 0], pe[:, :, :, 1], sin, ALU.mult))
            link(V.tensor_tensor(tr4[:, :, :, 1], pe[:, :, :, 0], sin, ALU.mult))
            link(V.tensor_tensor(ro[:, :, :, 0], ro[:, :, :, 0], tr4[:, :, :, 0], ALU.subtract))
            dve.wait_ge(s_kq, 1)
            V.tensor_tensor(ro[:, :, :, 1], ro[:, :, :, 1], tr4[:, :, :, 1], ALU.add).then_inc(s_kq, 1)
            link(V.tensor_scalar(iw[:, :, :], pj[:, :, CIW:CIW + IH], IW_SCALE, None, ALU.mult))
            dve.wait_ge(s_rexp, 2)
            link(V.tensor_reduce(small[:, 304:312], ex, AX, ALU.add))
            link(V.reciprocal(small[:, 304:312], small[:, 304:312]))
            link(V.tensor_tensor(ex, ex, small[:, 304:312].unsqueeze(2).broadcast_to([P, NT, E]), ALU.mult))
            t8 = tmp[:, 0:NT, 64:72]
            i8 = tmp[:, 0:NT, 72:80].bitcast(U32)
            f8 = tmp[:, 0:NT, 80:88]
            for t in range(NT):
                link(V.max(t8[:, t, :], ex[:, t, :]))
                link(V.max_index(i8[:, t, :], t8[:, t, :], ex[:, t, :]))
            link(V.tensor_copy(f8, i8))
            dve.wait_ge(s_init, 4)
            link(V.tensor_copy(small[:, 40:48], small[:, 312:320].bitcast(mybir.dt.int32)))
            it = small[:, 40:48].unsqueeze(1).broadcast_to([P, NT, E])
            sm12 = small[:, 304:312]
            link(V.tensor_tensor(sm12, t8[:, :, 0], t8[:, :, 1], ALU.add))
            link(V.reciprocal(sm12, sm12))
            link(V.tensor_scalar(sm12, sm12, LORA_SCALE, None, ALU.mult))
            link(V.tensor_tensor(t8[:, :, 0:2], t8[:, :, 0:2], sm12.unsqueeze(2).broadcast_to([P, NT, 2]), ALU.mult))
            we = tmp[:, :, 96:104]
            w1 = tmp[:, :, 104:112]
            link(V.tensor_tensor(we, it, f8[:, :, 0:1].broadcast_to([P, NT, E]), ALU.is_equal))
            link(V.tensor_tensor(we, we, t8[:, :, 0:1].broadcast_to([P, NT, E]), ALU.mult))
            link(V.tensor_tensor(w1, it, f8[:, :, 1:2].broadcast_to([P, NT, E]), ALU.is_equal))
            link(V.tensor_tensor(w1, w1, t8[:, :, 1:2].broadcast_to([P, NT, E]), ALU.mult))
            link(V.tensor_tensor(we, we, w1, ALU.add))
            V.tensor_tensor(hw, pj[:, :, CLO:CLO + E * R].rearrange("p t (e r) -> p t e r", e=E),
                            we.unsqueeze(3).broadcast_to([P, NT, E, R]), ALU.mult).then_inc(s_hw, 1)
            for t in range(NT):
                dve.wait_ge(s_bt, t + 1)
                V.tensor_tensor(gate[:, t, :], psS[:, t % 2, 0:HID], bias, ALU.add).then_inc(s_y, 1)
                if t:
                    finish_gate(dve, link, t - 1)
            finish_gate(dve, link, NT - 1)
            with dve.Fori(0, NP) as p:
                dve.wait_ge(s_wm, p * 4 + 4)
                V.tensor_scalar(Wvo[:, bass.ds(p * HID, HID)], psO[:, 0, :], wkv2[:, 0:1], None, ALU.mult).then_inc(s_wbfree, 1)

            def round_max(k, t):
                a = acc[:, acc_at(t):acc_at(t) + extent(t)]
                return V.max(top8[:, k, :], a)

            def round_take(k, t):
                a = acc[:, acc_at(t):acc_at(t) + extent(t)]
                return V.match_replace(a, top8[:, k, :], a, TAKEN)

            def masks(s, tiles):
                for t in tiles:
                    V.tensor_scalar(maskb[:, mask_at(t):mask_at(t) + extent(t)], acc[:, acc_at(t):acc_at(t) + extent(t)],
                                    BAR, MASKED, ALU.is_ge, ALU.mult).then_inc(s["mask"], 1)

            dve.wait_ge(s_accz, NT)
            for g in range(NG):
                s = IX[g]
                tiles = [t for t in range(GT * g, GT * g + GT) if t]
                n = len(tiles)
                prev = [t for t in range(GT * (g - 1), GT * g) if t]

                def accumulate(i, slot, first):
                    head = i * 2 + slot
                    for k, t in enumerate(tiles):
                        idx = i * (2 * n) + (slot * n + k)
                        dve.wait_ge(s["relu"], idx + 1)
                        if not (first and slot == 0):
                            dve.wait_ge(s["acc"], idx - n + 1)
                        a = acc[:, acc_at(t):acc_at(t) + extent(t)]
                        sc = iw[:, t, head:head + 1] if isinstance(head, int) else iw[:, t, bass.ds(head, 1)]
                        V.scalar_tensor_tensor(a, Sm[:, (slot * n + k) % 2, 0:extent(t)], sc, a, ALU.mult, ALU.add).then_inc(s["acc"], 1)
                    if g:
                        m = len(prev)
                        for k, t in enumerate(prev):
                            if not (first and slot == 0):
                                dve.wait_ge(s["top"], i * (4 * m) + (2 * m * slot - m + k + 1))
                                own(dve)
                            round_max(k, t).then_inc(s["top"], 1)
                        for k, t in enumerate(prev):
                            dve.wait_ge(s["top"], i * (4 * m) + (2 * m * slot + k + 1))
                            own(dve)
                            round_take(k, t).then_inc(s["top"], 1)

                if g:
                    dve.wait_ge(IX[0]["acc"], IH * (GT - 1))
                accumulate(0, 0, True)
                accumulate(0, 1, True)
                with dve.Fori(1, IH // 2) as i:
                    accumulate(i, 0, False)
                    accumulate(i, 1, False)
            dve.wait_ge(IX[1]["top"], 2 * (GT - 1) * ROUNDS)
            masks(IX[1], range(1, GT))
            dve.wait_ge(IX[1]["mask"], GT - 1)
            dve.wait_ge(IX[1]["acc"], IH * GT)

            for g in range(NG):
                s = AT[g]
                seq = uses(g)
                chunks = plan(g)
                nch = len(chunks)
                late = list(range(GT, NT))
                cols = slice(g * GW, (g + 1) * GW)

                def masked(p, j, first):
                    t = GT * g + j % GT
                    n = extent(t)
                    dve.wait_ge(s["sc"], p * 8 + (j + 1))
                    if not (first and j < 2):
                        dve.wait_ge(s["exp"], p * 8 + (j - 1))
                    own(dve)
                    V.tensor_tensor_reduce(Sm[:, j % 2, 0:n], psS[:, j % 2, 0:n], maskb[:, mask_at(t):mask_at(t) + n],
                                           -SCALE, 3.0e38, ALU.add, ALU.min, nmax[:, j:j + 1]).then_inc(s["masked"], 1)

                def norm(p, h, first):
                    dve.wait_ge(s["on"], p * nch + nch // 2 * (h + 1))
                    o = psO[:, h, :].rearrange("p (t a n) -> p t a n", t=GT, a=2)
                    V.reciprocal(rden[:, GT * h:GT * h + GT], den[:, GT * h:GT * h + GT]).then_inc(s["ln"], 1)
                    V.tensor_copy(osum[:, h, :, :], o[:, :, 1, :]).then_inc(s["ln"], 1)
                    dve.wait_ge(s["ln"], p * 6 + (3 * h + 2))
                    V.tensor_tensor(osum[:, h, :, :], o[:, :, 0, :], osum[:, h, :, :], ALU.add).then_inc(s["ln"], 1)
                    dve.wait_ge(s["ln"], p * 6 + (3 * h + 3))
                    if not first and h == 0:
                        dve.wait_ge(s["otr"], p)
                    V.tensor_tensor(On[:, :, h, :], osum[:, h, :, :],
                                    rden[:, GT * h:GT * h + GT].unsqueeze(2).broadcast_to([P, GT, KVR]),
                                    ALU.mult).then_inc(s["onrm"], 1)

                def body(p, first, last):
                    for u, (kind, c, j) in enumerate(seq):
                        bank = u % 2
                        if kind == "chunk" and (c == 0 or chunks[c - 1][0] != j):
                            if j < 6:
                                masked(p, j + 2, first)
                            elif not last:
                                masked(p + 1, j - 6, False)
                        if kind in ("pe", "sw"):
                            if not last:
                                dst, tab = (m1, ropeC) if kind == "pe" else (m2, ropeS)
                                dve.wait_ge(s["qp"], p * 3 + (5 if kind == "pe" else 6))
                                dve.wait_ge(s["qb"], p * 2 + 2)
                                V.tensor_tensor(dst[:, :], psT[:, bank, :], tab[:, cols], ALU.mult).then_inc(s["m12"], 1)
                        elif kind == "chunk":
                            nb = chunks[c][5]
                            dve.wait_ge(s["hi"], p * nch + (c + 1))
                            V.tensor_tensor(PTl[:, c % NBUF, 0:nb * P], psT[:, bank, 0:nb * P], PTh[:, c % NBUF, 0:nb * P],
                                            ALU.subtract).then_inc(s["lo"], 1)
                            done = c - LAG
                            if done == nch // 2 - 1:
                                norm(p, 0, first)
                            elif done + nch == nch - 1 and not first:
                                norm(p - 1, 1, False)
                            if g == 0 and (c == 0 or chunks[c - 1][0] != j):
                                k = j // 2
                                if j % 2 == 0:
                                    if not first:
                                        dve.wait_ge(IX[0]["top"], p * 8 + (j - 6))
                                        own(dve)
                                    round_max(k, late[k]).then_inc(IX[0]["top"], 1)
                                else:
                                    dve.wait_ge(IX[0]["top"], p * 8 + j)
                                    own(dve)
                                    round_take(k, late[k]).then_inc(IX[0]["top"], 1)

                if g:
                    masks(IX[0], late)
                    dve.wait_ge(IX[0]["mask"], GT)
                for k, (dst, tab) in enumerate(((m1, ropeC), (m2, ropeS))):
                    dve.wait_ge(s["qp"], 2 + k)
                    V.tensor_tensor(dst[:, :], psT[:, 1 - k, :], tab[:, cols], ALU.mult).then_inc(s["m12"], 1)
                masked(0, 0, True)
                masked(0, 1, True)
                body(0, True, False)
                with dve.Fori(1, NP - 1) as p:
                    body(p, False, False)
                body(NP - 1, False, True)
                norm(NP - 1, 1, False)
                if g == 0:
                    dve.wait_ge(IX[0]["top"], 2 * GT * ROUNDS)

            for t in range(NT):
                dve.wait_ge(s_fin, t + 1)
                dve.wait_ge((s_fd0, s_fd1)[t % 2], 32 * (t // 2 + 1))
                dst = (m1 if t % 2 == 0 else m2)[:, :]
                if t >= 2:
                    dve.wait_ge((s_fo0, s_fo1)[t % 2], 16 * (t // 2))
                V.tensor_tensor(dst, psO[:, t % 2, :], Sm[:, t % 2, HID:2 * HID], ALU.mult).then_inc(s_fy, 1)
                dve.wait_ge(s_fy, t + 1)
                V.tensor_tensor(dst, dst, Sm[:, t % 2, 0:HID], ALU.add).then_inc(s_fadd, 1)

        @block.tensor
        def _(pe):
            T = nc.tensor

            def bank_read(s, seq, nch, p, u, first, last):
                v = u - 2
                while v >= 0 and (seq[v][0] in ("c", "pe", "sw") and last or seq[v][0] == "o" and first):
                    v -= 2
                if v < 0 and first:
                    pe.wait_ge(s["m12"], 2)
                    return
                kind, c, _ = seq[v % len(seq)]
                q = p if v >= 0 else p - 1
                if kind == "c":
                    pe.wait_ge(s["cps"], q + 2)
                elif kind in ("pe", "sw"):
                    pe.wait_ge(s["m12"], q * 2 + (3 if kind == "pe" else 4))
                elif kind == "o":
                    pe.wait_ge(s["ot"], q)
                else:
                    pe.wait_ge(s["lo"], q * nch + (c + 1))

            def mm(out, lhsT, rhs, start=True, stop=True):
                return T.matmul(out, lhsT, rhs, start=start, stop=stop)

            pe.wait_ge(s_ident, 1)
            pe.wait_ge(s_w, 16)
            for t in range(NT + 1):
                if t < NT:
                    pe.wait_ge(s_xn, t + 1)
                    if t >= 2:
                        pe.wait_ge(s_xc, t - 1)
                    for c in range(HC):
                        last = T.transpose(psT[:, t % 2, c * P:(c + 1) * P], xin[:, t, c * P:(c + 1) * P], ident[:, :])
                    last.then_inc(s_xt, 1)
                if t:
                    u = t - 1
                    pe.wait_ge(s_xc, u + 1)
                    if u >= 2:
                        pe.wait_ge(s_pjc, u - 1)
                    for c in range(HC):
                        last = mm(psO[:, u % 2, 0:NPROJ], xnT[:, c, u * P:(u + 1) * P], wproj[:, c, :], c == 0, c == HC - 1)
                    last.then_inc(s_pj, 1)
            pe.wait_ge(s_w2, 16)
            pe.wait_ge(s_w2, 16 * 11)
            for k in range(2):
                for c in range(HC):
                    last = mm(psS[:, 0, k * 512:(k + 1) * 512], wslot[:, 0, c, :], xnT[:, c, k * 512:(k + 1) * 512], c == 0, c == HC - 1)
                last.then_inc(s_ik, 1)
            pe.wait_ge(s_kq, 2)
            for t in range(NT):
                if t >= 2:
                    pe.wait_ge(s_ktc, 4 * (t - 1))
                T.transpose(psT[:, t % 2, 0:P], kbuf[:, t, 0:128], ident[:, :])
                T.transpose(psT[:, t % 2, P:2 * P], kbuf[:, t, 64:192], ident[:, :])
                T.transpose(psT[:, t % 2, 2 * P:3 * P], qn[:, t, 0:P], ident[:, :])
                T.transpose(psT[0:QR - P, t % 2, 3 * P:4 * P], qn[:, t, P:QR], ident[:, :]).then_inc(s_kt, 1)
            pe.wait_ge(s_hw, 1)
            pe.wait_ge(s_pjc, NT)
            for t in range(NT):
                if t >= 2:
                    pe.wait_ge(s_hwc, t - 1)
                T.transpose(psO[:, t % 2, 0:P], Sm[:, 0, t * P:(t + 1) * P], ident[:, :]).then_inc(s_hwt, 1)
            pe.wait_ge(s_ikc, 2)
            for t in range(NT):
                pe.wait_ge(s_hwc, t + 1)
                if t >= 2:
                    pe.wait_ge(s_y, t - 1)
                for c in range(HC):
                    mm(psS[:, t % 2, 0:HID], xnT[:, c, t * P:(t + 1) * P], WbT[:, c, :], c == 0, False)
                mm(psS[:, t % 2, 0:HID], hwT[:, t * P:(t + 1) * P], loraB, False, True).then_inc(s_bt, 1)
            pe.wait_ge(s_ktc, 4 * NT)

            def head_weights(p, k, first):
                dst = wslot[:, k, :, :].rearrange("p c n -> p (c n)")
                pe.wait_ge((s_wd0, s_wd1)[k], p * 32 + 32)
                if not first:
                    pe.wait_ge(s_wcc, p * 4 + (2 * k - 2))
                wk, wv = dst[:, QR:QR + KVR], dst[:, QR + KVR:QR + 2 * KVR]
                mm(psT[:, k, 0:64], dst[:, 0:P], wk)
                mm(psT[0:QR - P, k, 64:128], dst[:, P:QR], wk).then_inc(s_wm, 1)
                if not first and k == 0:
                    pe.wait_ge(s_wbfree, p)
                mm(psO[64 * k:64 * k + 64, 0, :], wv, qAB[:, k, :]).then_inc(s_wm, 1)

            for k in range(2):
                head_weights(0, k, True)
            with pe.Fori(1, NP) as p:
                for k in range(2):
                    head_weights(p, k, False)
            pe.wait_ge(s_wcc, 2 * H)
            pe.wait_ge(s_wbfree, NP)
            pe.wait_ge(s_y, NT)
            for g in range(NG):
                s = IX[g]
                tiles = [t for t in range(GT * g, GT * g + GT) if t]
                n = len(tiles)

                def project(i, slot, first):
                    pe.wait_ge(s[f"dma{slot}"], i * 16 + 16)
                    if not first:
                        pe.wait_ge(s["qc"], i * 2 + (slot - 1))
                    for c in range(HC):
                        last = mm(psT[:, slot, :], wslot[:, slot, c, :], xnT[:, c, g * GW:(g + 1) * GW], c == 0, c == HC - 1)
                    last.then_inc(s["q"], 1)

                def score(i, slot, first):
                    pe.wait_ge(s["qc"], i * 2 + (slot + 1))
                    for k, t in enumerate(tiles):
                        idx = i * (2 * n) + (slot * n + k)
                        b = (slot * n + k) % 2
                        if not (first and slot * n + k < 2):
                            pe.wait_ge(s["relu"], idx - 1)
                        q = qAB[:, slot, (t % GT) * P:(t % GT + 1) * P]
                        for lo in range(0, extent(t), 512):
                            hi = min(lo + 512, extent(t))
                            last = mm(psS[:, b, lo:hi], q, ikT[:, lo:hi])
                        last.then_inc(s["sc"], 1)

                if g:
                    pe.wait_ge(IX[0]["relu"], IH * (GT - 1))
                    pe.wait_ge(IX[0]["qc"], IH)
                project(0, 0, True)
                project(0, 1, True)
                score(0, 0, True)
                with pe.Fori(1, IH // 2) as i:
                    project(i, 0, False)
                    score(i - 1, 1, False)
                    project(i, 1, False)
                    score(i, 0, False)
                score(IH // 2 - 1, 1, False)
            pe.wait_ge(IX[1]["relu"], IH * GT)
            for g in range(NG):
                s = AT[g]
                seq = uses(g)
                chunks = plan(g)
                nch = len(chunks)
                cols = slice(g * GW, (g + 1) * GW)

                def queries(bank, part):
                    mm(psT[:, bank, :], stage1[:, part, :], qT1[:, cols], True, False)
                    return mm(psT[:, bank, :], stage2[:, part, :], qT2[:, cols], False, True)

                def score(p, j, first):
                    h, t = j // GT, GT * g + j % GT
                    if j == 0:
                        pe.wait_ge(s["qa"], p * 2 + 2)
                    if j == GT:
                        pe.wait_ge(s["qb"], p * 2 + 2)
                    if not (first and j < 2):
                        pe.wait_ge(s["masked"], p * 8 + (j - 1))
                    keys = KF if h else KT
                    q = qAB[:, h, (j % GT) * P:(j % GT + 1) * P]
                    for lo in range(0, extent(t), 512):
                        hi = min(lo + 512, extent(t))
                        last = mm(psS[:, j % 2, lo:hi], q, keys[:, lo:hi])
                    last.then_inc(s["sc"], 1)

                def latent(p, c, first):
                    j, h, slot, t, b0, nb, ends = chunks[c]
                    pe.wait_ge(s["lo"], p * nch + (c + 1))
                    if c in (0, nch // 2) and not first:
                        pe.wait_ge(s["onrm"], p * 2 + (h - 1))
                    o = psO[:, h, slot * P:(slot + 1) * P]
                    for k in range(nb):
                        b = b0 + k
                        T.matmul(o, PTh[:, c % NBUF, k * P:(k + 1) * P], Vhl[:, b, :, :].rearrange("p a n -> p (a n)"),
                                 start=(b == 0), stop=(b == t))
                        last = T.matmul(o[:, 0:KVR], PTl[:, c % NBUF, k * P:(k + 1) * P], Vhl[:, b, 0, :],
                                        start=False, stop=False, skip_group_check=True)
                    last.then_inc(s["on"], 1)

                def body(p, first, last):
                    for u, (kind, c, j) in enumerate(seq):
                        bank = u % 2
                        if kind == "chunk" and (c == 0 or chunks[c - 1][0] != j):
                            if j < 6:
                                score(p, j + 2, first)
                            elif not last:
                                score(p + 1, j - 6, False)
                        if kind in ("c", "pe", "sw") and last or kind == "o" and first:
                            continue
                        bank_read(s, seq, nch, p, u, first, last)
                        if kind in ("c", "pe", "sw"):
                            if kind == "c":
                                pe.wait_ge(s["dma"], p * 64 + 128)
                            queries(bank, ("c", "pe", "sw").index(kind)).then_inc(s["qp"], 1)
                        elif kind == "o":
                            outputs(bank, p - 1).then_inc(s["otr"], 1)
                        else:
                            _, h, slot, t, b0, nb, ends = chunks[c]
                            if c == 0 or chunks[c - 1][0] != j:
                                pe.wait_ge(s["exp"], p * 8 + (j + 1))
                            for k in range(nb):
                                m = T.transpose(psT[:, bank, k * P:(k + 1) * P],
                                                Pr[:, j % 2, (b0 + k) * P:(b0 + k + 1) * P], ident[:, :])
                            m.then_inc(s["pt"], 1)
                            if c >= LAG:
                                latent(p, c - LAG, first)
                            elif not first:
                                latent(p - 1, nch + c - LAG, False)

                def outputs(bank, p):
                    pe.wait_ge(s["onrm"], p * 2 + 2)
                    for k in range(GT):
                        m = T.transpose(psT[:, bank, k * P:(k + 1) * P], On[:, k, :, :].rearrange("p a n -> p (a n)"), ident[:, :])
                    return m

                if g:
                    pe.wait_ge(AT[0]["ot"], NP)
                pe.wait_ge(s["dma"], 64)
                queries(0, 0).then_inc(s["qp"], 1)
                queries(1, 1).then_inc(s["qp"], 1)
                pe.wait_ge(s["cps"], 1)
                queries(0, 2).then_inc(s["qp"], 1)
                pe.wait_ge(s["m12"], 2)
                score(0, 0, True)
                score(0, 1, True)
                body(0, True, False)
                with pe.Fori(1, NP - 1) as p:
                    body(p, False, False)
                body(NP - 1, False, True)
                for c in range(nch - LAG, nch):
                    latent(NP - 1, c, False)
                pe.wait_ge(s["lo"], NP * nch)
                outputs(0, NP - 1).then_inc(s["otr"], 1)
            pe.wait_ge(AT[1]["ot"], NP)
            for t in range(NT):
                if t >= 2:
                    pe.wait_ge(s_fadd, t - 1)
                for p in range(NP):
                    last = mm(psO[:, t % 2, :], OTv[:, p, t * P:(t + 1) * P], Wvo[:, p * HID:(p + 1) * HID], p == 0, p == NP - 1)
                last.then_inc(s_fin, 1)


def kernel(**inputs):
    import numpy as np
    import concourse.bacc as bacc
    from concourse.bass_utils import run_bass_kernel_spmd as run

    f = {k.replace("L0_", ""): np.asarray(v) for k, v in inputs.items()}
    x = f["attn_hidden_states"].reshape(S, HID)
    qb = f["attn_q_b_w"].reshape(QR, H, NOPE + ROPE)
    kvb = f["attn_kv_b_w"].reshape(KVR, H, NOPE + VD)
    headw = np.concatenate([qb[:, :, :NOPE].transpose(1, 2, 0), kvb[:, :, :NOPE].transpose(1, 2, 0),
                            kvb[:, :, NOPE:].transpose(1, 2, 0)], axis=2)
    qpe = qb[:, :, NOPE:].reshape(QR, NP, 2, ROPE)[:, :, ::-1]
    swapped = qpe.reshape(QR, NP, 2, ROPE // 2, 2)[..., ::-1].reshape(QR, NP, 2, ROPE)
    pairw = np.stack([qpe, swapped], axis=2).reshape(QR, NP, 2, P).transpose(1, 0, 2, 3)
    inv = (np.float32(1.0) / np.float32(10000.0) ** (np.arange(0, ROPE, 2, dtype=np.float32) / np.float32(ROPE))).astype(np.float32)
    ang = np.arange(S, dtype=np.float32)[:, None] * inv[None, :]
    cos, sin = np.cos(ang).astype(np.float32), np.sin(ang).astype(np.float32)
    ropeC = np.tile(np.repeat(cos.T, 2, axis=0), (2, 1))
    ropeS = np.tile(np.stack([-sin.T, sin.T], axis=1).reshape(ROPE, S), (2, 1))
    arrays = {
        "x": x,
        "wproj": np.concatenate([f["attn_q_a_w"], f["attn_kv_a_w"], f["attn_idx_weights_w"], f["ffn_W_router"].T,
                                 f["ffn_lora_A"].reshape(E * R, HID).T], axis=1),
        "ik_w": f["attn_idx_wk_w"], "iq_w": f["attn_idx_wq_w"],
        "wq_norm": f["attn_q_a_norm_w"], "wkv_norm": f["attn_kv_a_norm_w"],
        "ktab": np.stack([cos, sin], axis=1), "ropeC": ropeC, "ropeS": ropeS,
        "b_base": f["ffn_b_base"], "lora_B": f["ffn_lora_B"].transpose(0, 2, 1).reshape(E * R, HID),
        "WbT": f["ffn_W_base"].T, "headw": headw, "o_w": f["attn_o_w"], "pairw": pairw,
    }
    nc = bacc.Bacc("TRN2", target_bir_lowering=False, num_devices=1)
    named, aps = {}, {}
    for name, a in arrays.items():
        a = np.ascontiguousarray(a)
        named[f"in_{name}"] = a
        aps[name] = nc.dram_tensor(f"in_{name}", a.shape, mybir.dt.from_np(a.dtype), kind="ExternalInput").ap()
    aps["out"] = nc.dram_tensor("out_0", (S, HID), F32, kind="ExternalOutput").ap()
    build(nc, aps)
    r = run(nc, [named], core_ids=[0])
    return r.results[0]["out_0"].reshape(1, S, HID)
```

```python
from contextlib import ExitStack

import concourse.bass as bass
from concourse import mybir

F32 = mybir.dt.float32
F16 = mybir.dt.float16
BF16 = mybir.dt.bfloat16
U32 = mybir.dt.uint32
ALU = mybir.AluOpType
ACT = mybir.ActivationFunctionType
AX = mybir.AxisListType.X

P = 128
S, HID = 1024, 512
NT = S // P
GT = 4
GW = GT * P
NG = NT // GT
HC = HID // P
H, NOPE, ROPE, VD = 32, 128, 64, 128
QR, KVR = 192, 64
NP = H // 2
IH, ID, TOPK = 16, 128, 128
E, R = 8, 16
EPS = 1e-5
CQ, CKV, CPE, CIW, CRT, CLO = 0, QR, QR + KVR, QR + KVR + ROPE, QR + KVR + ROPE + IH, QR + KVR + ROPE + IH + E
NPROJ = CLO + E * R
SCALE = float(NOPE + ROPE) ** -0.5
IW_SCALE = float(IH) ** -0.5 * float(ID) ** -0.5
LORA_SCALE = 2.0
FUTURE = -3.0e38
TAKEN = -3.4e38
BAR = -3.2e38
MASKED = -1.0e30
ROUNDS = TOPK // 8
SLOTS = 4
TOP_INDEX = {4: 2, 5: 2}
TOP_WEIGHTS = {1: 2, 2: 2, 3: 2}
TOP_ATTEND = {6: 1, 7: 1}
LATE = min(TOP_ATTEND)
LAG = 2
NBUF = 4
EXTRA = {0: ("c", 0), 1: ("pe", 0), 3: ("o", 0), 5: ("o", 1)}
SWAP = [i ^ 1 for i in range(32)]


def extent(t):
    return (t + 1) * P


def acc_at(t):
    return sum(extent(k) for k in range(1, t))


def mask_at(t):
    return sum(extent(k) for k in range(t))


def splits(t):
    n = t + 1
    if n <= 4:
        return [(0, n)]
    return [(0, (n + 1) // 2), ((n + 1) // 2, n // 2)]


def plan(g):
    out = []
    for j in range(2 * GT):
        t = GT * g + j % GT
        parts = splits(t)
        for n, (b0, nb) in enumerate(parts):
            out.append((j, j // GT, j % GT, t, b0, nb, n == len(parts) - 1))
    return out


def uses(g):
    chunks = plan(g)
    out = []
    for j in range(2 * GT):
        if j in EXTRA:
            out.append(EXTRA[j] + (j,))
        for c, ch in enumerate(chunks):
            if ch[0] == j:
                out.append(("chunk", c, j))
    return out


def rounds(per):
    ops = []
    for k in range(max(per.values())):
        now = [t for t in per if per[t] > k]
        ops += [(t, True) for t in now] + [(t, False) for t in now]
    out = []
    for n, (t, is_max) in enumerate(ops):
        before = [m for m in range(n) if ops[m] == (t, not is_max)]
        last = [m for m in range(len(ops)) if ops[m] == (t, not is_max)]
        out.append((t, is_max, (before or last)[-1], bool(before)))
    return out


def transposed(g, p, j):
    chunks = plan(g)
    q = p if j >= 0 else p - 1
    return q * len(chunks) + (1 + max(c for c, ch in enumerate(chunks) if ch[0] == j % 8))


def build(nc, A):
    with ExitStack() as ctx:
        def sb(name, shape, dt=F32):
            return ctx.enter_context(nc.sbuf_tensor(name, shape, dt))

        def psum(name, shape):
            return ctx.enter_context(nc.psum_tensor(name, shape, F32))

        def sem(name):
            return ctx.enter_context(nc.semaphore(name))

        psS = psum("psS", [P, 2, 1024])
        psT = psum("psT", [P, 2, 512])
        psO = psum("psO", [P, 2, 512])

        OT = sb("OT", [P, NP * S])
        OTv = OT[:, :].rearrange("p (n s) -> p n s", n=NP)
        Wvo = sb("Wvo", [P, NP * HID])
        Wc1 = sb("Wc1", [P, NP * P])
        low = sb("low", [P, NP * P])
        Wc2 = low[0:QR - P, :]
        qT2 = low[QR - P:P, 0:S]
        stage2 = low[QR - P:P, S:S + 2 * P].rearrange("p (a n) -> p a n", a=2)
        KT = sb("KT", [P, S])
        KF = sb("KF", [P, S])
        ikT = sb("ikT", [P, S])
        qT1 = sb("qT1", [P, S])
        acc = sb("acc", [P, acc_at(NT)])
        maskb = sb("maskb", [P, mask_at(NT)], BF16)
        Vhl = sb("Vhl", [P, NT, 2, KVR], F16)
        iw = sb("iw", [P, NT, IH])
        ropeC = sb("ropeC", [P, S])
        ropeS = sb("ropeS", [P, S])
        ident = sb("ident", [P, P])
        stage1 = sb("stage1", [P, 2, P])
        wslot = sb("wslot", [P, 2, HC, P])
        Sm = sb("Sm", [P, 2, S])
        Pr = sb("Pr", [P, 2, S])
        PTh = sb("PTh", [P, NBUF, 512], F16)
        PTl = sb("PTl", [P, NBUF, 512], F16)
        qAB = sb("qAB", [P, 2, GW])
        cT = ikT[:, 0:GW]
        m1 = ikT[:, GW:2 * GW]
        m2 = sb("m2", [P, GW])
        nmax = sb("nmax", [P, 2 * GT])
        den = sb("den", [P, 2 * GT])
        rden = sb("rden", [P, 2 * GT])
        osum = sb("osum", [P, 2, GT, KVR])
        On = sb("On", [P, GT, 2, KVR])
        top8 = sb("top8", [P, NT, 8])
        small = sb("small", [P, 320])
        wkv2 = sb("wkv2", [P, 1])

        def early(lo, n):
            return OT[:, lo:lo + n]

        at = 0
        xin = early(at, NT * HID).rearrange("p (t d) -> p t d", t=NT); at += NT * HID
        pj = early(at, NT * NPROJ).rearrange("p (t n) -> p t n", t=NT); at += NT * NPROJ
        xnT = early(at, HC * S).rearrange("p (c s) -> p c s", c=HC); at += HC * S
        wproj = early(at, HC * NPROJ).rearrange("p (c n) -> p c n", c=HC); at += HC * NPROJ
        ktab = early(at, NT * ROPE).rearrange("p (t a n) -> p t a n", t=NT, a=2); at += NT * ROPE
        wqb = early(at, QR); at += QR
        wkvb = early(at, KVR); at += KVR
        assert at <= NP * S
        xnT_dram = nc.dram_tensor("xnT_scratch", [P, HC * S], F32, kind="Internal").ap()
        hwT_dram = nc.dram_tensor("hwT_scratch", [P, S], F32, kind="Internal").ap()
        hwT = Pr[:, 0, :]
        hwsb = Wvo[:, NT * 704:NT * 832]
        hw = hwsb.rearrange("p (t e r) -> p t e r", t=NT, e=E)
        kbuf = Wvo[:, 0:NT * 192].rearrange("p (t n) -> p t n", t=NT)
        qn = Wvo[:, NT * 192:NT * 384].rearrange("p (t n) -> p t n", t=NT)
        latn = Wvo[:, NT * 384:NT * 448].rearrange("p (t n) -> p t n", t=NT)
        tmp = Wvo[:, NT * 448:NT * (448 + 192)].rearrange("p (t n) -> p t n", t=NT)
        ktmp = Wvo[:, NT * 640:NT * 704].rearrange("p (t n) -> p t n", t=NT)
        hslot = [b[:, 2 * k:2 * k + 2, :].bitcast(F32).rearrange("p a n -> p (a n)") for b in (PTh, PTl) for k in range(2)]
        oslot = [Pr[:, k // 2, (k % 2) * HID:(k % 2) * HID + HID] for k in range(SLOTS)]
        gxnT = acc[:, 0:HC * S].rearrange("p (c s) -> p c s", c=HC)
        WbT = Wc1[:, :].rearrange("p (c n) -> p c n", c=HC)
        ghwT = low[:, 0:S]
        loraB = low[:, S:S + HID]
        bias = low[:, S + HID:S + 2 * HID]

        def following(g, p, last):
            if not last:
                return g, p + 1
            return (g + 1, 0) if g + 1 < NG else None

        def sems(names):
            return [sem(n) for n in names.split()]

        (s_w, s_w2, s_ident, s_mv, s_sd, s_xn, s_xt, s_xc, s_pj, s_pjc, s_ik, s_ikc, s_kq, s_kt, s_ktc,
         s_vec, s_rexp, s_sq, s_rms, s_pool, s_iw, s_hw, s_hwt, s_hwc, s_spill, s_accz,
         s_wm, s_wcc, s_wvc, s_init, s_passed) = sems(
            "s_w s_w2 s_ident s_mv s_sd s_xn s_xt s_xc s_pj s_pjc s_ik s_ikc s_kq s_kt s_ktc "
            "s_vec s_rexp s_sq s_rms s_pool s_iw s_hw s_hwt s_hwc s_spill s_accz "
            "s_wm s_wcc s_wvc s_init s_passed")
        s_wd = [sem(f"s_wd{k}") for k in range(SLOTS)]
        s_topi, s_topw, s_topa, s_mask0, s_mask1 = sems("s_topi s_topw s_topa s_mask0 s_mask1")

        block = ctx.enter_context(nc.Block())

        def W(eng, s, v):
            if isinstance(v, int) and v <= 0:
                return
            eng.wait_ge(s, v)

        def own(eng):
            eng.sem_inc(s_passed, 1)

        s_x = [sem(f"s_x{t}") for t in range(NT)]
        IX = [dict(zip("dma0 dma1 q qc sc relu acc".split(),
                       sems(" ".join(f"ix{g}_{n}" for n in "dma0 dma1 q qc sc relu acc".split()))))
              for g in range(NG)]
        AT = [dict(zip("dma qp qa qb sc masked exp pt cps m1 m2 rot hi lo on onrm otr ot ln".split(),
                       sems(" ".join(f"at{g}_{n}" for n in
                                     "dma qp qa qb sc masked exp pt cps m1 m2 rot hi lo on onrm otr ot ln".split()))))
              for g in range(NG)]
        (s_gload, s_gm, s_gy, s_ge, s_gg, s_gp, s_fin, s_fd0, s_fd1, s_fo0, s_fo1, s_fadd) = sems(
            "s_gload s_gm s_gy s_ge s_gg s_gp s_fin s_fd0 s_fd1 s_fo0 s_fo1 s_fadd")

        def yout(t):
            return Sm[:, t % 2, HID:2 * HID]

        def load_head(sp, slot, h):
            sp.dma_start(hslot[slot][:, 0:QR + 2 * KVR],
                         A["headw"][bass.ds(h, 1)].rearrange("a p n -> p (a n)")).then_inc(s_wd[slot], 16)
            sp.dma_start(oslot[slot], A["o_w"][bass.ds(h * VD, VD), :]).then_inc(s_wd[slot], 16)

        def load_index(sp, s, slot, n):
            sp.dma_start(wslot[:, slot, :, :],
                         A["iq_w"].rearrange("(c p) n -> p c n", p=P)[:, :, bass.ds(n * ID, ID)]).then_inc(s[f"dma{slot}"], 16)

        def load_pair(sp, s, p):
            sp.dma_start(stage1[:, 1, :], A["pairw"][bass.ds(p, 1), 0:P].rearrange("a r n -> (a r) n")).then_inc(s["dma"], 16)
            sp.dma_start(stage2[:, 1, :], A["pairw"][bass.ds(p, 1), P:QR].rearrange("a r n -> (a r) n")).then_inc(s["dma"], 16)
            sp.dma_start(stage1[:, 0, :], Wc1[:, bass.ds(p * P, P)]).then_inc(s["dma"], 16)
            sp.dma_start(stage2[:, 0, :], Wc2[:, bass.ds(p * P, P)]).then_inc(s["dma"], 16)

        @block.sync
        def _(sp):
            for t in range(NT):
                sp.dma_start(xin[:, t, :], A["x"][t * P:(t + 1) * P, :]).then_inc(s_x[t], 16)
                if t == 0:
                    sp.dma_start(wproj, A["wproj"].rearrange("(c p) n -> p c n", p=P)).then_inc(s_w, 16)
            sp.dma_start(wslot[:, 0, :, :], A["ik_w"].rearrange("(c p) n -> p c n", p=P)).then_inc(s_w2, 16)
            for dst, src in ((wqb, A["wq_norm"].partition_broadcast(P)), (wkvb, A["wkv_norm"].partition_broadcast(P)),
                             (ktab, A["ktab"].rearrange("(t p) a n -> p t a n", p=P)),
                             (wkv2[0:KVR, :], A["wkv_norm"].rearrange("(n a) -> n a", a=1)),
                             (wkv2[KVR:P, :], A["wkv_norm"].rearrange("(n a) -> n a", a=1)),
                             (ropeC[:, :], A["ropeC"]), (ropeS[:, :], A["ropeS"])):
                sp.dma_start(dst, src).then_inc(s_w2, 16)
            for g in (1, 0):
                s = IX[g]
                if g:
                    sp.wait_ge(s_ikc, 2)
                    load_index(sp, s, 0, 0)
                    load_index(sp, s, 1, 1)
                    sp.wait_ge(s_xc, NT)
                    sp.dma_start(xnT_dram, xnT.rearrange("p c s -> p (c s)")).then_inc(s_spill, 16)
                else:
                    sp.wait_ge(IX[1]["q"], IH)
                    load_index(sp, s, 0, 0)
                    load_index(sp, s, 1, 1)
                    sp.wait_ge(s_hwc, NT)
                    sp.dma_start(hwT_dram, hwT).then_inc(s_spill, 16)
                with sp.Fori(1, IH // 2) as i:
                    for slot in range(2):
                        sp.wait_ge(s["q"], i * 2 + (slot - 1))
                        load_index(sp, s, slot, i * 2 + slot)
            sp.wait_ge(s_spill, 32)
            for slot in range(SLOTS):
                load_head(sp, slot, slot)
            sp.wait_ge(s_wcc, 4)
            load_pair(sp, AT[0], 0)
            with sp.Fori(1, H // SLOTS) as i:
                for slot in range(SLOTS):
                    sp.wait_ge(s_wm, i * (2 * SLOTS) + (2 * slot + 2 - 2 * SLOTS))
                    load_head(sp, slot, i * SLOTS + slot)
            for g in range(NG):
                s = AT[g]
                if g:
                    sp.wait_ge(AT[0]["qp"], 2 * NP)
                    load_pair(sp, s, 0)
                else:
                    sp.wait_ge(s_wcc, 2 * H)
                with sp.Fori(1, NP) as p:
                    sp.wait_ge(s["qp"], p * 2)
                    load_pair(sp, s, p)
            sp.wait_ge(AT[1]["qp"], 2 * NP)
            for dst, src in ((gxnT.rearrange("p c s -> p (c s)"), xnT_dram), (ghwT, hwT_dram), (loraB, A["lora_B"]),
                             (bias, A["b_base"].partition_broadcast(P)),
                             (WbT, A["WbT"].rearrange("(c p) n -> p c n", p=P))):
                sp.dma_start(dst, src).then_inc(s_gload, 16)
            sp.wait_ge(AT[1]["exp"], NP * 2 * GT)
            for t in range(NT):
                if t >= 2:
                    sp.wait_ge(s_fadd, t - 1)
                    sp.dma_start(A["out"][(t - 2) * P:(t - 1) * P, :], yout(t)).then_inc((s_fo0, s_fo1)[t % 2], 16)
                sp.dma_start(Sm[:, t % 2, 0:HID], A["x"][t * P:(t + 1) * P, :]).then_inc((s_fd0, s_fd1)[t % 2], 16)
            for t in range(NT - 2, NT):
                sp.wait_ge(s_fadd, t + 1)
                sp.dma_start(A["out"][t * P:(t + 1) * P, :], yout(t)).then_inc((s_fo0, s_fo1)[t % 2], 16)
            sp.wait_ge(s_fo0, 16 * NT // 2)
            sp.wait_ge(s_fo1, 16 * NT // 2)

        @block.gpsimd
        def _(pool):
            nc.gpsimd.memset(ident[:, :], 0.0).then_inc(s_init, 1)
            nc.gpsimd.memset(acc[:, :], 0.0).then_inc(s_init, 1)
            nc.gpsimd.memset(maskb[:, 0:P], 0.0).then_inc(s_init, 1)
            nc.gpsimd.iota(small[:, 312:320].bitcast(mybir.dt.int32), pattern=[[1, E]], base=0, channel_multiplier=0).then_inc(s_init, 1)
            pool.wait_ge(s_init, 4)
            nc.gpsimd.affine_select(out=ident[:, :], in_=ident[:, :], compare_op=ALU.not_equal, fill=1.0,
                                    base=0, pattern=[[-1, P]], channel_multiplier=1).then_inc(s_ident, 1)
            nc.gpsimd.affine_select(out=maskb[:, 0:P], in_=maskb[:, 0:P], compare_op=ALU.is_ge, fill=MASKED,
                                    base=0, pattern=[[-1, P]], channel_multiplier=1).then_inc(s_accz, 1)
            for t in range(1, NT):
                d = acc[:, acc_at(t) + t * P:acc_at(t) + (t + 1) * P]
                nc.gpsimd.affine_select(out=d, in_=d, compare_op=ALU.is_ge, fill=FUTURE,
                                        base=0, pattern=[[-1, P]], channel_multiplier=1).then_inc(s_accz, 1)

            G = nc.gpsimd
            np_ = [0]

            def link(ins):
                np_[0] += 1
                ins.then_inc(s_pool, 1)
                pool.wait_ge(s_pool, np_[0])

            rq, rk = small[:, 64:72], small[:, 72:80]
            pool.wait_ge(s_rms, 1)
            pool.wait_ge(s_w2, 16 * 8)
            pool.wait_ge(s_pjc, NT)
            link(G.tensor_tensor(latn, pj[:, :, CKV:CKV + KVR], rk.unsqueeze(2).broadcast_to([P, NT, KVR]), ALU.mult))
            wk3 = wkvb.unsqueeze(1).broadcast_to([P, NT, KVR])
            link(G.tensor_tensor(kbuf[:, :, 0:KVR], latn, wk3, ALU.mult))
            link(G.tensor_tensor(kbuf[:, :, 128:192], latn, wk3, ALU.mult))
            link(G.tensor_copy(Vhl[:, :, 0, :], latn))
            link(G.tensor_tensor(Vhl[:, :, 1, :], latn, Vhl[:, :, 0, :], ALU.subtract))
            kp = pj[:, :, CPE:CPE + ROPE].rearrange("p t (i a) -> p t i a", a=2)
            ro = kbuf[:, :, KVR:KVR + ROPE].rearrange("p t (i a) -> p t i a", a=2)
            kt4 = ktmp.rearrange("p t (i a) -> p t i a", a=2)
            cos, sin = ktab[:, :, 0, :], ktab[:, :, 1, :]
            link(G.tensor_tensor(ro[:, :, :, 0], kp[:, :, :, 0], cos, ALU.mult))
            link(G.tensor_tensor(ro[:, :, :, 1], kp[:, :, :, 1], cos, ALU.mult))
            link(G.tensor_tensor(kt4[:, :, :, 0], kp[:, :, :, 1], sin, ALU.mult))
            link(G.tensor_tensor(kt4[:, :, :, 1], kp[:, :, :, 0], sin, ALU.mult))
            link(G.tensor_tensor(ro[:, :, :, 0], ro[:, :, :, 0], kt4[:, :, :, 0], ALU.subtract))
            link(G.tensor_tensor(ro[:, :, :, 1], ro[:, :, :, 1], kt4[:, :, :, 1], ALU.add))
            link(G.tensor_tensor(qn, pj[:, :, 0:QR], rq.unsqueeze(2).broadcast_to([P, NT, QR]), ALU.mult))
            G.tensor_tensor(qn, qn, wqb.unsqueeze(1).broadcast_to([P, NT, QR]), ALU.mult).then_inc(s_kq, 1)

            def before(g, s, p, left):
                if not isinstance(p, int):
                    pool.wait_ge(s["sc"], p * 8 - left)
                elif g:
                    pool.wait_ge(AT[g - 1]["sc"], NP * 8 - left)

            def queries(g, s, cols, p):
                pool.wait_ge(s["m2"], p + 1)
                nc.gpsimd.tensor_tensor(m2[:, :], m2[:, :], ropeS[:, cols], ALU.mult).then_inc(s["rot"], 1)
                pool.wait_ge(s["cps"], p + 1)
                before(g, s, p, 4)
                own(pool)
                nc.gpsimd.tensor_copy(qAB[0:64, 0, :], cT[0:64, :]).then_inc(s["qa"], 1)
                pool.wait_ge(s["m1"], p + 1)
                pool.wait_ge(s["rot"], p + 1)
                nc.gpsimd.tensor_tensor(qAB[64:P, 0, :], m1[64:P, :], m2[64:P, :], ALU.add).then_inc(s["qa"], 1)
                before(g, s, p, 0)
                own(pool)
                nc.gpsimd.tensor_copy(qAB[64:P, 1, :], cT[64:P, :]).then_inc(s["qb"], 1)
                nc.gpsimd.tensor_tensor(qAB[0:64, 1, :], m1[0:64, :], m2[0:64, :], ALU.add).then_inc(s["qb"], 1)

            pool.wait_ge(IX[0]["sc"], IH * (GT - 1))
            for g in range(NG):
                s = AT[g]
                cols = slice(g * GW, (g + 1) * GW)
                queries(g, s, cols, 0)
                with pool.Fori(1, NP) as p:
                    queries(g, s, cols, p)

        def act_index(act, g):
            s = IX[g]
            tiles = [t for t in range(GT * g, GT * g + GT) if t]
            n = len(tiles)

            def head(i, slot, first):
                act.wait_ge(s["q"], i * 2 + (slot + 1))
                if not first:
                    act.wait_ge(s["sc"], i * (2 * n) + (slot * n - n))
                nc.scalar.activation(qAB[:, slot, :], psT[:, slot, :], ACT.Copy).then_inc(s["qc"], 1)
                for k, t in enumerate(tiles):
                    idx = i * (2 * n) + (slot * n + k)
                    act.wait_ge(s["sc"], idx + 1)
                    if not (first and slot * n + k < 2):
                        act.wait_ge(s["acc"], idx - 1)
                    b = (slot * n + k) % 2
                    nc.scalar.activation(Sm[:, b, 0:extent(t)], psS[:, b, 0:extent(t)], ACT.Relu).then_inc(s["relu"], 1)

            if g == 0:
                act.wait_ge(IX[1]["acc"], IH * GT)
            head(0, 0, True)
            head(0, 1, True)
            with act.Fori(1, IH // 2) as i:
                head(i, 0, False)
                head(i, 1, False)
        @block.scalar
        def _(act):
            act.wait_ge(s_mv, 1)
            nc.scalar.activation(small[:, 24:32], small[:, 16:24], ACT.Sqrt).then_inc(s_sd, 1)
            for t in range(NT):
                act.wait_ge(s_xt, t + 1)
                nc.scalar.activation(xnT[:, :, t * P:(t + 1) * P], psT[:, t % 2, :].rearrange("p (c n) -> p c n", c=HC),
                                     ACT.Copy).then_inc(s_xc, 1)
                act.wait_ge(s_pj, t + 1)
                nc.scalar.activation(pj[:, t, :], psO[:, t % 2, 0:NPROJ], ACT.Copy).then_inc(s_pjc, 1)
            act.wait_ge(s_sq, 1)
            nc.scalar.activation(small[:, 64:80], small[:, 48:64], ACT.Sqrt).then_inc(s_sd, 1)
            for k in range(2):
                act.wait_ge(s_ik, k + 1)
                nc.scalar.activation(ikT[:, k * 512:(k + 1) * 512], psS[:, 0, k * 512:(k + 1) * 512], ACT.Copy).then_inc(s_ikc, 1)
            act.wait_ge(s_rexp, 1)
            nc.scalar.activation(small[:, 88:152], small[:, 88:152], ACT.Exp).then_inc(s_rexp, 1)
            act_index(act, 1)
            for t in range(NT):
                act.wait_ge(s_kt, t + 1)
                c = slice(t * P, (t + 1) * P)
                nc.scalar.activation(KT[:, c], psT[:, t % 2, 0:P], ACT.Copy).then_inc(s_ktc, 1)
                nc.scalar.activation(KF[:, c], psT[:, t % 2, P:2 * P], ACT.Copy).then_inc(s_ktc, 1)
                nc.scalar.activation(qT1[:, c], psT[:, t % 2, 2 * P:3 * P], ACT.Copy).then_inc(s_ktc, 1)
                nc.scalar.activation(qT2[:, c], psT[0:QR - P, t % 2, 3 * P:4 * P], ACT.Copy).then_inc(s_ktc, 1)
            for t in range(NT):
                act.wait_ge(s_hwt, t + 1)
                nc.scalar.activation(hwT[:, t * P:(t + 1) * P], psO[:, t % 2, 0:P], ACT.Copy).then_inc(s_hwc, 1)
            act_index(act, 0)
            def weights_out(i):
                for k in range(SLOTS):
                    h = i * SLOTS + k
                    act.wait_ge(s_wm, i * (2 * SLOTS) + (2 * k + 1))
                    nc.scalar.activation(Wc1[:, bass.ds(h * 64, 64)], psT[:, k % 2, 0:64], ACT.Copy).then_inc(s_wcc, 1)
                    nc.scalar.activation(Wc2[:, bass.ds(h * 64, 64)], psT[0:QR - P, k % 2, 64:128], ACT.Copy).then_inc(s_wcc, 1)
                    if k % 2:
                        act.wait_ge(s_wm, i * (2 * SLOTS) + (2 * k + 2))
                        nc.scalar.activation(Wvo[:, bass.ds((h - 1) * (HID // 2), HID)], psO[:, k // 2, :], ACT.Copy,
                                             scale=wkv2[:, 0:1]).then_inc(s_wvc, 1)

            weights_out(0)
            act.wait_ge(AT[0]["qp"], 1)
            nc.scalar.activation(cT[:, :], psS[:, 0, 0:GW], ACT.Copy).then_inc(AT[0]["cps"], 1)
            with act.Fori(1, H // SLOTS) as i:
                weights_out(i)
            for g in range(NG):
                s = AT[g]
                seq = uses(g)
                chunks = plan(g)
                nch = len(chunks)

                def exp(p, j, first, last_of_prev=False):
                    act.wait_ge(s["masked"], p * 8 + (j + 1))
                    if not (first and j < 2):
                        act.wait_ge(s["pt"], transposed(g, p, j - 2))
                    if not first and j % GT == 0:
                        act.wait_ge(s["onrm"], p * 2 + (j // GT - 1))
                    t = GT * g + j % GT
                    nc.scalar.activation(Pr[:, j % 2, 0:extent(t)], Sm[:, j % 2, 0:extent(t)], ACT.Exp,
                                         bias=nmax[:, j:j + 1], scale=-1.0, accum_out=den[:, j:j + 1]).then_inc(s["exp"], 1)

                def body(p, first, last):
                    for u, (kind, c, j) in enumerate(seq):
                        bank = u % 2
                        if kind == "chunk" and (c == 0 or chunks[c - 1][0] != j):
                            if j < 7:
                                exp(p, j + 1, first)
                            elif not last:
                                exp(p + 1, 0, False)
                        if kind == "c":
                            nxt = following(g, p, last)
                            if nxt:
                                act.wait_ge(AT[nxt[0]]["qp"], nxt[1] * 2 + 1)
                                act.wait_ge(s["qb"], p * 2 + 2)
                                nc.scalar.activation(cT[:, :], psT[:, bank, :], ACT.Copy).then_inc(AT[nxt[0]]["cps"], 1)
                        elif kind == "o" and not first:
                            act.wait_ge(s["otr"], p * 2 + (c - 1))
                            nc.scalar.activation(OT[:, bass.ds((p - 1) * S + (g * GW + c * GW // 2), GW // 2)],
                                                 psT[:, bank, 0:GW // 2], ACT.Copy).then_inc(s["ot"], 1)
                        elif kind == "chunk":
                            nb = chunks[c][5]
                            act.wait_ge(s["pt"], p * nch + (c + 1))
                            if not (first and c < NBUF):
                                act.wait_ge(s["on"], p * nch + (c - NBUF + 1))
                            nc.scalar.activation(PTh[:, c % NBUF, 0:nb * P], psT[:, bank, 0:nb * P], ACT.Copy).then_inc(s["hi"], 1)

                if g:
                    act.wait_ge(AT[0]["onrm"], 2 * NP)
                else:
                    act.wait_ge(s_spill, 32)
                exp(0, 0, True)
                body(0, True, False)
                with act.Fori(1, NP - 1) as p:
                    body(p, False, False)
                body(NP - 1, False, True)
                for c in range(2):
                    act.wait_ge(s["otr"], 2 * NP - 1 + c)
                    at = (NP - 1) * S + g * GW + c * GW // 2
                    nc.scalar.activation(OT[:, at:at + GW // 2], psT[:, c, 0:GW // 2], ACT.Copy).then_inc(s["ot"], 1)
            for t in range(NT):
                act.wait_ge(s_gy, t + 1)
                nc.scalar.activation(Pr[:, t % 2, 0:HID], Pr[:, t % 2, HID:2 * HID], ACT.Exp, scale=-1.0).then_inc(s_ge, 1)

        @block.vector
        def _(dve):
            nv = [0]
            V = nc.vector

            def link(ins):
                nv[0] += 1
                ins.then_inc(s_vec, 1)
                dve.wait_ge(s_vec, nv[0])

            def rsqrt_refine(out, x, y, t1):
                link(V.reciprocal(t1, y))
                link(V.tensor_tensor(out, t1, t1, ALU.mult))
                link(V.tensor_tensor(out, out, x, ALU.mult))
                link(V.tensor_scalar(out, out, -0.5, 1.5, ALU.mult, ALU.add))
                link(V.tensor_tensor(out, out, t1, ALU.mult))

            for t in range(NT):
                dve.wait_ge(s_x[t], 16)
                link(V.bn_stats(small[:, 160 + 6 * t:166 + 6 * t], xin[:, t, :]))
                link(V.bn_aggr(small[:, 2 * t:2 * t + 2], small[:, 160 + 6 * t:166 + 6 * t]))
            mv = small[:, 0:16].rearrange("p (t a) -> p t a", a=2)
            V.tensor_scalar(small[:, 16:24], mv[:, :, 1], EPS, None, ALU.add).then_inc(s_mv, 1)
            dve.wait_ge(s_sd, 1)
            dve.wait_ge(s_mv, 1)
            rsqrt_refine(small[:, 32:40], small[:, 16:24], small[:, 24:32], small[:, 40:48])
            for t in range(NT):
                V.tensor_scalar(xin[:, t, :], xin[:, t, :], small[:, 2 * t:2 * t + 1], small[:, 32 + t:33 + t],
                                ALU.subtract, ALU.mult).then_inc(s_xn, 1)
            dve.wait_ge(s_pjc, NT)
            link(V.tensor_tensor(tmp, pj[:, :, 0:QR], pj[:, :, 0:QR], ALU.mult))
            link(V.tensor_reduce(small[:, 48:56], tmp, AX, ALU.add))
            link(V.tensor_tensor(tmp[:, :, 0:KVR], pj[:, :, CKV:CKV + KVR], pj[:, :, CKV:CKV + KVR], ALU.mult))
            link(V.tensor_reduce(small[:, 56:64], tmp[:, :, 0:KVR], AX, ALU.add))
            link(V.tensor_scalar(small[:, 48:56], small[:, 48:56], 1.0 / QR, EPS, ALU.mult, ALU.add))
            V.tensor_scalar(small[:, 56:64], small[:, 56:64], 1.0 / KVR, EPS, ALU.mult, ALU.add).then_inc(s_sq, 1)
            lg = pj[:, :, CRT:CRT + E]
            ex = small[:, 88:152].rearrange("p (t e) -> p t e", t=NT)
            link(V.tensor_reduce(small[:, 80:88], lg, AX, ALU.max))
            V.tensor_tensor(ex, lg, small[:, 80:88].unsqueeze(2).broadcast_to([P, NT, E]), ALU.subtract).then_inc(s_rexp, 1)
            link(V.tensor_scalar(iw[:, :, :], pj[:, :, CIW:CIW + IH], IW_SCALE, None, ALU.mult))
            dve.wait_ge(s_sd, 2)
            dve.wait_ge(s_sq, 1)
            rsqrt_refine(small[:, 64:80], small[:, 48:64], small[:, 64:80], small[:, 288:304])
            dve.sem_inc(s_rms, 1)
            dve.wait_ge(s_rexp, 2)
            link(V.tensor_reduce(small[:, 304:312], ex, AX, ALU.add))
            link(V.reciprocal(small[:, 304:312], small[:, 304:312]))
            link(V.tensor_tensor(ex, ex, small[:, 304:312].unsqueeze(2).broadcast_to([P, NT, E]), ALU.mult))
            t8 = tmp[:, 0:NT, 64:72]
            i8 = tmp[:, 0:NT, 72:80].bitcast(U32)
            f8 = tmp[:, 0:NT, 80:88]
            for t in range(NT):
                link(V.max(t8[:, t, :], ex[:, t, :]))
                link(V.max_index(i8[:, t, :], t8[:, t, :], ex[:, t, :]))
            link(V.tensor_copy(f8, i8))
            dve.wait_ge(s_init, 4)
            link(V.tensor_copy(small[:, 40:48], small[:, 312:320].bitcast(mybir.dt.int32)))
            it = small[:, 40:48].unsqueeze(1).broadcast_to([P, NT, E])
            sm12 = small[:, 304:312]
            link(V.tensor_tensor(sm12, t8[:, :, 0], t8[:, :, 1], ALU.add))
            link(V.reciprocal(sm12, sm12))
            link(V.tensor_scalar(sm12, sm12, LORA_SCALE, None, ALU.mult))
            link(V.tensor_tensor(t8[:, :, 0:2], t8[:, :, 0:2], sm12.unsqueeze(2).broadcast_to([P, NT, 2]), ALU.mult))
            we = tmp[:, :, 96:104]
            w1 = tmp[:, :, 104:112]
            link(V.tensor_tensor(we, it, f8[:, :, 0:1].broadcast_to([P, NT, E]), ALU.is_equal))
            link(V.tensor_tensor(we, we, t8[:, :, 0:1].broadcast_to([P, NT, E]), ALU.mult))
            link(V.tensor_tensor(w1, it, f8[:, :, 1:2].broadcast_to([P, NT, E]), ALU.is_equal))
            link(V.tensor_tensor(w1, w1, t8[:, :, 1:2].broadcast_to([P, NT, E]), ALU.mult))
            link(V.tensor_tensor(we, we, w1, ALU.add))
            V.tensor_tensor(hw, pj[:, :, CLO:CLO + E * R].rearrange("p t (e r) -> p t e r", e=E),
                            we.unsqueeze(3).broadcast_to([P, NT, E, R]), ALU.mult).then_inc(s_hw, 1)
            def top(s_top, per, it, op, first):
                ops = rounds(per)
                t, is_max, before, here = ops[op]
                if here or not first:
                    dve.wait_ge(s_top, (it if here else it - 1) * len(ops) + (before + 1))
                    if not isinstance(it, int):
                        own(dve)
                a = acc[:, acc_at(t):acc_at(t) + extent(t)]
                ins = V.max(top8[:, t, :], a) if is_max else V.match_replace(a, top8[:, t, :], a, TAKEN)
                ins.then_inc(s_top, 1)

            def masks(s_mask, tiles):
                for t in tiles:
                    V.tensor_scalar(maskb[:, mask_at(t):mask_at(t) + extent(t)], acc[:, acc_at(t):acc_at(t) + extent(t)],
                                    BAR, MASKED, ALU.is_ge, ALU.mult).then_inc(s_mask, 1)

            dve.wait_ge(s_accz, NT)
            for g in (1, 0):
                s = IX[g]
                tiles = [t for t in range(GT * g, GT * g + GT) if t]
                n = len(tiles)

                def accumulate(i, slot, first):
                    head = i * 2 + slot
                    for k, t in enumerate(tiles):
                        idx = i * (2 * n) + (slot * n + k)
                        dve.wait_ge(s["relu"], idx + 1)
                        if not (first and slot == 0):
                            dve.wait_ge(s["acc"], idx - n + 1)
                        a = acc[:, acc_at(t):acc_at(t) + extent(t)]
                        sc = iw[:, t, head:head + 1] if isinstance(head, int) else iw[:, t, bass.ds(head, 1)]
                        V.scalar_tensor_tensor(a, Sm[:, (slot * n + k) % 2, 0:extent(t)], sc, a, ALU.mult, ALU.add).then_inc(s["acc"], 1)
                    if g == 0:
                        half = len(rounds(TOP_INDEX)) // 2
                        for op in range(half * slot, half * slot + half):
                            top(s_topi, TOP_INDEX, i, op, first)

                if g == 0:
                    dve.wait_ge(IX[1]["acc"], IH * GT)
                accumulate(0, 0, True)
                accumulate(0, 1, True)
                with dve.Fori(1, IH // 2) as i:
                    accumulate(i, 0, False)
                    accumulate(i, 1, False)
            def rope(g, pe_out):
                own(dve)
                V.stream_shuffle(m2[:, :], pe_out, SWAP).then_inc(AT[g]["m2"], 1)
                V.tensor_tensor(m1[:, :], pe_out, ropeC[:, g * GW:(g + 1) * GW], ALU.mult).then_inc(AT[g]["m1"], 1)

            n = len(rounds(TOP_WEIGHTS))
            dve.wait_ge(IX[0]["acc"], IH * (GT - 1))
            dve.wait_ge(s_topi, len(rounds(TOP_INDEX)) * (IH // 2))
            for op in range(n):
                top(s_topw, TOP_WEIGHTS, 0, op, True)
            dve.wait_ge(AT[0]["qp"], 2)
            rope(0, psS[:, 1, 0:GW])
            with dve.Fori(1, ROUNDS // 2) as i:
                for op in range(n):
                    top(s_topw, TOP_WEIGHTS, i, op, False)
            dve.wait_ge(s_topw, n * (ROUNDS // 2))
            masks(s_mask0, range(1, LATE))
            dve.wait_ge(s_mask0, LATE - 1)

            for g in range(NG):
                s = AT[g]
                seq = uses(g)
                chunks = plan(g)
                nch = len(chunks)

                def masked(p, j, first):
                    t = GT * g + j % GT
                    n = extent(t)
                    dve.wait_ge(s["sc"], p * 8 + (j + 1))
                    if not (first and j < 2):
                        dve.wait_ge(s["exp"], p * 8 + (j - 1))
                    own(dve)
                    V.tensor_tensor_reduce(Sm[:, j % 2, 0:n], psS[:, j % 2, 0:n], maskb[:, mask_at(t):mask_at(t) + n],
                                           -SCALE, 3.0e38, ALU.add, ALU.min, nmax[:, j:j + 1]).then_inc(s["masked"], 1)

                def norm(p, h, first):
                    dve.wait_ge(s["on"], p * nch + nch // 2 * (h + 1))
                    o = psO[:, h, :].rearrange("p (t a n) -> p t a n", t=GT, a=2)
                    V.reciprocal(rden[:, GT * h:GT * h + GT], den[:, GT * h:GT * h + GT]).then_inc(s["ln"], 1)
                    V.tensor_copy(osum[:, h, :, :], o[:, :, 1, :]).then_inc(s["ln"], 1)
                    dve.wait_ge(s["ln"], p * 6 + (3 * h + 2))
                    V.tensor_tensor(osum[:, h, :, :], o[:, :, 0, :], osum[:, h, :, :], ALU.add).then_inc(s["ln"], 1)
                    dve.wait_ge(s["ln"], p * 6 + (3 * h + 3))
                    if not first and h == 0:
                        dve.wait_ge(s["otr"], p * 2)
                    V.tensor_tensor(On[:, :, h, :], osum[:, h, :, :],
                                    rden[:, GT * h:GT * h + GT].unsqueeze(2).broadcast_to([P, GT, KVR]),
                                    ALU.mult).then_inc(s["onrm"], 1)

                def body(p, first, last):
                    for u, (kind, c, j) in enumerate(seq):
                        bank = u % 2
                        if kind == "chunk" and (c == 0 or chunks[c - 1][0] != j):
                            if j < 6:
                                masked(p, j + 2, first)
                            elif not last:
                                masked(p + 1, j - 6, False)
                        if kind == "pe":
                            nxt = following(g, p, last)
                            if nxt:
                                dve.wait_ge(AT[nxt[0]]["qp"], nxt[1] * 2 + 2)
                                dve.wait_ge(s["qb"], p * 2 + 2)
                                rope(nxt[0], psT[:, bank, :])
                        elif kind == "chunk":
                            nb = chunks[c][5]
                            dve.wait_ge(s["hi"], p * nch + (c + 1))
                            V.tensor_tensor(PTl[:, c % NBUF, 0:nb * P], psT[:, bank, 0:nb * P], PTh[:, c % NBUF, 0:nb * P],
                                            ALU.subtract).then_inc(s["lo"], 1)
                            done = c - LAG
                            if done == nch // 2 - 1:
                                norm(p, 0, first)
                            elif done + nch == nch - 1 and not first:
                                norm(p - 1, 1, False)
                            every = 2 * GT // len(rounds(TOP_ATTEND))
                            if g == 0 and j % every == 0 and (c == 0 or chunks[c - 1][0] != j):
                                top(s_topa, TOP_ATTEND, p, j // every, first)

                if g:
                    dve.wait_ge(s_topa, len(rounds(TOP_ATTEND)) * ROUNDS)
                    masks(s_mask1, range(LATE, NT))
                    dve.wait_ge(s_mask1, NT - LATE)
                masked(0, 0, True)
                masked(0, 1, True)
                body(0, True, False)
                with dve.Fori(1, NP - 1) as p:
                    body(p, False, False)
                body(NP - 1, False, True)
                norm(NP - 1, 1, False)

            dve.wait_ge(s_gload, 16 * 5)
            for t in range(NT + 1):
                if t < NT:
                    if t >= 2:
                        dve.wait_ge(s_ge, t - 1)
                    dve.wait_ge(s_gm, t + 1)
                    V.tensor_tensor(Pr[:, t % 2, HID:2 * HID], psS[:, t % 2, 0:HID], bias, ALU.add).then_inc(s_gy, 1)
                if t:
                    u = t - 1
                    e, y = Pr[:, u % 2, 0:HID], Pr[:, u % 2, HID:2 * HID]
                    dve.wait_ge(s_ge, u + 1)
                    link(V.tensor_scalar(e, e, 1.0, None, ALU.add))
                    link(V.reciprocal(e, e))
                    link(V.tensor_tensor(e, e, y, ALU.mult))
                    dve.wait_ge(s_fin, u + 1)
                    if u >= 2:
                        dve.wait_ge((s_fo0, s_fo1)[u % 2], 16 * (u // 2))
                    link(V.tensor_tensor(yout(u), psO[:, u % 2, :], e, ALU.mult))
                    dve.wait_ge((s_fd0, s_fd1)[u % 2], 16 * (u // 2 + 1))
                    V.tensor_tensor(yout(u), yout(u), Sm[:, u % 2, 0:HID], ALU.add).then_inc(s_fadd, 1)

        @block.tensor
        def _(pe):
            T = nc.tensor

            def bank_read(g, s, seq, nch, p, u, first, last):
                v = u - 2
                nxt = following(g, p, last)
                while v >= 0 and (seq[v][0] in ("c", "pe") and not nxt or seq[v][0] == "o" and first):
                    v -= 2
                if v < 0 and first:
                    return
                kind, c, _ = seq[v % len(seq)]
                q = p if v >= 0 else p - 1
                if kind == "c":
                    pe.wait_ge(AT[nxt[0]]["cps"], nxt[1] + 1)
                elif kind == "pe":
                    pe.wait_ge(AT[nxt[0]]["m1"], nxt[1] + 1)
                elif kind == "o":
                    pe.wait_ge(s["ot"], q * 2 + (c - 1))
                else:
                    pe.wait_ge(s["lo"], q * nch + (c + 1))

            def mm(out, lhsT, rhs, start=True, stop=True):
                return T.matmul(out, lhsT, rhs, start=start, stop=stop)

            pe.wait_ge(s_ident, 1)
            pe.wait_ge(s_w, 16)
            for t in range(NT + 1):
                if t < NT:
                    pe.wait_ge(s_xn, t + 1)
                    if t >= 2:
                        pe.wait_ge(s_xc, t - 1)
                    for c in range(HC):
                        last = T.transpose(psT[:, t % 2, c * P:(c + 1) * P], xin[:, t, c * P:(c + 1) * P], ident[:, :])
                    last.then_inc(s_xt, 1)
                if t:
                    u = t - 1
                    pe.wait_ge(s_xc, u + 1)
                    if u >= 2:
                        pe.wait_ge(s_pjc, u - 1)
                    for c in range(HC):
                        last = mm(psO[:, u % 2, 0:NPROJ], xnT[:, c, u * P:(u + 1) * P], wproj[:, c, :], c == 0, c == HC - 1)
                    last.then_inc(s_pj, 1)
            pe.wait_ge(s_w2, 16 * 8)
            for k in range(2):
                for c in range(HC):
                    last = mm(psS[:, 0, k * 512:(k + 1) * 512], wslot[:, 0, c, :], xnT[:, c, k * 512:(k + 1) * 512], c == 0, c == HC - 1)
                last.then_inc(s_ik, 1)
            def keys_and_latents():
                pe.wait_ge(s_kq, 1)
                pe.wait_ge(IX[1]["qc"], IH)
                for t in range(NT):
                    if t >= 2:
                        pe.wait_ge(s_ktc, 4 * (t - 1))
                    T.transpose(psT[:, t % 2, 0:P], kbuf[:, t, 0:128], ident[:, :])
                    T.transpose(psT[:, t % 2, P:2 * P], kbuf[:, t, 64:192], ident[:, :])
                    T.transpose(psT[:, t % 2, 2 * P:3 * P], qn[:, t, 0:P], ident[:, :])
                    T.transpose(psT[0:QR - P, t % 2, 3 * P:4 * P], qn[:, t, P:QR], ident[:, :]).then_inc(s_kt, 1)
                pe.wait_ge(s_hw, 1)
                for t in range(NT):
                    if t >= 2:
                        pe.wait_ge(s_hwc, t - 1)
                    T.transpose(psO[:, t % 2, 0:P], hwsb[:, t * P:(t + 1) * P], ident[:, :]).then_inc(s_hwt, 1)
                pe.wait_ge(s_ktc, 4 * NT)

            for g in (1, 0):
                if g == 0:
                    keys_and_latents()
                s = IX[g]
                tiles = [t for t in range(GT * g, GT * g + GT) if t]
                n = len(tiles)

                def project(i, slot, first):
                    pe.wait_ge(s[f"dma{slot}"], i * 16 + 16)
                    if not first:
                        pe.wait_ge(s["qc"], i * 2 + (slot - 1))
                    for c in range(HC):
                        last = mm(psT[:, slot, :], wslot[:, slot, c, :], xnT[:, c, g * GW:(g + 1) * GW], c == 0, c == HC - 1)
                    last.then_inc(s["q"], 1)

                def score(i, slot, first):
                    pe.wait_ge(s["qc"], i * 2 + (slot + 1))
                    for k, t in enumerate(tiles):
                        idx = i * (2 * n) + (slot * n + k)
                        b = (slot * n + k) % 2
                        if not (first and slot * n + k < 2):
                            pe.wait_ge(s["relu"], idx - 1)
                        q = qAB[:, slot, (t % GT) * P:(t % GT + 1) * P]
                        for lo in range(0, extent(t), 512):
                            hi = min(lo + 512, extent(t))
                            last = mm(psS[:, b, lo:hi], q, ikT[:, lo:hi])
                        last.then_inc(s["sc"], 1)

                if g == 0:
                    pe.wait_ge(IX[1]["relu"], IH * GT)
                project(0, 0, True)
                project(0, 1, True)
                score(0, 0, True)
                with pe.Fori(1, IH // 2) as i:
                    project(i, 0, False)
                    score(i - 1, 1, False)
                    project(i, 1, False)
                    score(i, 0, False)
                score(IH // 2 - 1, 1, False)
            pe.wait_ge(IX[0]["relu"], IH * (GT - 1))

            def head_weights(i, k, first):
                dst = hslot[k]
                pe.wait_ge(s_wd[k], i * 32 + 32)
                if not (first and k < 2):
                    pe.wait_ge(s_wcc, i * (2 * SLOTS) + (2 * k - 2))
                wk, wv = dst[:, QR:QR + KVR], dst[:, QR + KVR:QR + 2 * KVR]
                mm(psT[:, k % 2, 0:64], dst[:, 0:P], wk)
                mm(psT[0:QR - P, k % 2, 64:128], dst[:, P:QR], wk).then_inc(s_wm, 1)
                if not first and k % 2 == 0:
                    pe.wait_ge(s_wvc, i * 2 + (k // 2 - 1))
                mm(psO[64 * (k % 2):64 * (k % 2) + 64, k // 2, :], wv, oslot[k]).then_inc(s_wm, 1)

            def queries(g, out, part):
                cols = slice(g * GW, (g + 1) * GW)
                mm(out, stage1[:, part, :], qT1[:, cols], True, False)
                mm(out, stage2[:, part, :], qT2[:, cols], False, True).then_inc(AT[g]["qp"], 1)

            for k in range(SLOTS):
                head_weights(0, k, True)
            pe.wait_ge(AT[0]["dma"], 64)
            queries(0, psS[:, 0, 0:GW], 0)
            queries(0, psS[:, 1, 0:GW], 1)
            with pe.Fori(1, H // SLOTS) as i:
                for k in range(SLOTS):
                    head_weights(i, k, False)
            pe.wait_ge(s_wcc, 2 * H)
            pe.wait_ge(s_wvc, NP)
            for g in range(NG):
                s = AT[g]
                seq = uses(g)
                chunks = plan(g)
                nch = len(chunks)

                def score(p, j, first):
                    h, t = j // GT, GT * g + j % GT
                    if j == 0:
                        pe.wait_ge(s["qa"], p * 2 + 2)
                    if j == GT:
                        pe.wait_ge(s["qb"], p * 2 + 2)
                    if not (first and j < 2):
                        pe.wait_ge(s["masked"], p * 8 + (j - 1))
                    keys = KF if h else KT
                    q = qAB[:, h, (j % GT) * P:(j % GT + 1) * P]
                    for lo in range(0, extent(t), 512):
                        hi = min(lo + 512, extent(t))
                        last = mm(psS[:, j % 2, lo:hi], q, keys[:, lo:hi])
                    last.then_inc(s["sc"], 1)

                def latent(p, c, first):
                    j, h, slot, t, b0, nb, ends = chunks[c]
                    pe.wait_ge(s["lo"], p * nch + (c + 1))
                    if c in (0, nch // 2) and not first:
                        pe.wait_ge(s["onrm"], p * 2 + (h - 1))
                    o = psO[:, h, slot * P:(slot + 1) * P]
                    for k in range(nb):
                        b = b0 + k
                        T.matmul(o, PTh[:, c % NBUF, k * P:(k + 1) * P], Vhl[:, b, :, :].rearrange("p a n -> p (a n)"),
                                 start=(b == 0), stop=(b == t))
                        last = T.matmul(o[:, 0:KVR], PTl[:, c % NBUF, k * P:(k + 1) * P], Vhl[:, b, 0, :],
                                        start=False, stop=False, skip_group_check=True)
                    last.then_inc(s["on"], 1)

                def body(p, first, last):
                    for u, (kind, c, j) in enumerate(seq):
                        bank = u % 2
                        if kind == "chunk" and (c == 0 or chunks[c - 1][0] != j):
                            if j < 6:
                                score(p, j + 2, first)
                            elif not last:
                                score(p + 1, j - 6, False)
                        nxt = following(g, p, last)
                        if kind in ("c", "pe") and not nxt or kind == "o" and first:
                            continue
                        bank_read(g, s, seq, nch, p, u, first, last)
                        if kind in ("c", "pe"):
                            if kind == "c":
                                pe.wait_ge(AT[nxt[0]]["dma"], nxt[1] * 64 + 64)
                            queries(nxt[0], psT[:, bank, :], ("c", "pe").index(kind))
                        elif kind == "o":
                            outputs(bank, p - 1, c).then_inc(s["otr"], 1)
                        else:
                            _, h, slot, t, b0, nb, ends = chunks[c]
                            if c == 0 or chunks[c - 1][0] != j:
                                pe.wait_ge(s["exp"], p * 8 + (j + 1))
                            for k in range(nb):
                                m = T.transpose(psT[:, bank, k * P:(k + 1) * P],
                                                Pr[:, j % 2, (b0 + k) * P:(b0 + k + 1) * P], ident[:, :])
                            m.then_inc(s["pt"], 1)
                            if c >= LAG:
                                latent(p, c - LAG, first)
                            elif not first:
                                latent(p - 1, nch + c - LAG, False)

                def outputs(bank, p, half):
                    pe.wait_ge(s["onrm"], p * 2 + 2)
                    for k in range(GT // 2):
                        m = T.transpose(psT[:, bank, k * P:(k + 1) * P], On[:, half * GT // 2 + k, :, :].rearrange("p a n -> p (a n)"), ident[:, :])
                    return m

                if g:
                    pe.wait_ge(AT[0]["ot"], 2 * NP)
                else:
                    pe.wait_ge(s["cps"], 1)
                    pe.wait_ge(s["m1"], 1)
                score(0, 0, True)
                score(0, 1, True)
                body(0, True, False)
                with pe.Fori(1, NP - 1) as p:
                    body(p, False, False)
                body(NP - 1, False, True)
                for c in range(nch - LAG, nch):
                    latent(NP - 1, c, False)
                pe.wait_ge(s["lo"], NP * nch)
                for half in range(2):
                    outputs(half, NP - 1, half).then_inc(s["otr"], 1)
            pe.wait_ge(AT[1]["ot"], 2 * NP)
            pe.wait_ge(s_gload, 16 * 5)
            for t in range(NT + 1):
                if t < NT:
                    if t >= 2:
                        pe.wait_ge(s_gy, t - 1)
                    else:
                        pe.wait_ge(AT[1]["masked"], NP * 2 * GT)
                    for c in range(HC):
                        mm(psS[:, t % 2, 0:HID], gxnT[:, c, t * P:(t + 1) * P], WbT[:, c, :], c == 0, False)
                    mm(psS[:, t % 2, 0:HID], ghwT[:, t * P:(t + 1) * P], loraB, False, True).then_inc(s_gm, 1)
                if t:
                    u = t - 1
                    if u >= 2:
                        pe.wait_ge(s_fadd, u - 1)
                    for p in range(NP):
                        last = mm(psO[:, u % 2, :], OTv[:, p, u * P:(u + 1) * P], Wvo[:, p * HID:(p + 1) * HID], p == 0, p == NP - 1)
                    last.then_inc(s_fin, 1)


def kernel(**inputs):
    import numpy as np
    import concourse.bacc as bacc
    from concourse.bass_utils import run_bass_kernel_spmd as run

    f = {k.replace("L0_", ""): np.asarray(v) for k, v in inputs.items()}
    x = f["attn_hidden_states"].reshape(S, HID)
    qb = f["attn_q_b_w"].reshape(QR, H, NOPE + ROPE)
    kvb = f["attn_kv_b_w"].reshape(KVR, H, NOPE + VD)
    headw = np.concatenate([qb[:, :, :NOPE].transpose(1, 2, 0), kvb[:, :, :NOPE].transpose(1, 2, 0),
                            kvb[:, :, NOPE:].transpose(1, 2, 0)], axis=2)
    qpe = qb[:, :, NOPE:].reshape(QR, NP, 2, ROPE)[:, :, ::-1]
    pairw = qpe.reshape(QR, NP, P).transpose(1, 0, 2)
    inv = (np.float32(1.0) / np.float32(10000.0) ** (np.arange(0, ROPE, 2, dtype=np.float32) / np.float32(ROPE))).astype(np.float32)
    ang = np.arange(S, dtype=np.float32)[:, None] * inv[None, :]
    cos, sin = np.cos(ang).astype(np.float32), np.sin(ang).astype(np.float32)
    ropeC = np.tile(np.repeat(cos.T, 2, axis=0), (2, 1))
    ropeS = np.tile(np.stack([-sin.T, sin.T], axis=1).reshape(ROPE, S), (2, 1))
    arrays = {
        "x": x,
        "wproj": np.concatenate([f["attn_q_a_w"], f["attn_kv_a_w"], f["attn_idx_weights_w"], f["ffn_W_router"].T,
                                 f["ffn_lora_A"].reshape(E * R, HID).T], axis=1),
        "ik_w": f["attn_idx_wk_w"], "iq_w": f["attn_idx_wq_w"],
        "wq_norm": f["attn_q_a_norm_w"], "wkv_norm": f["attn_kv_a_norm_w"],
        "ktab": np.stack([cos, sin], axis=1), "ropeC": ropeC, "ropeS": ropeS,
        "b_base": f["ffn_b_base"], "lora_B": f["ffn_lora_B"].transpose(0, 2, 1).reshape(E * R, HID),
        "WbT": f["ffn_W_base"].T, "headw": headw, "o_w": f["attn_o_w"], "pairw": pairw,
    }
    nc = bacc.Bacc("TRN2", target_bir_lowering=False, num_devices=1)
    named, aps = {}, {}
    for name, a in arrays.items():
        a = np.ascontiguousarray(a)
        named[f"in_{name}"] = a
        aps[name] = nc.dram_tensor(f"in_{name}", a.shape, mybir.dt.from_np(a.dtype), kind="ExternalInput").ap()
    aps["out"] = nc.dram_tensor("out_0", (S, HID), F32, kind="ExternalOutput").ap()
    build(nc, aps)
    r = run(nc, [named], core_ids=[0])
    return r.results[0]["out_0"].reshape(1, S, HID)
```

```python
from contextlib import ExitStack

import concourse.bass as bass
from concourse import mybir

F32 = mybir.dt.float32
F32R = mybir.dt.float32r
F16 = mybir.dt.float16
BF16 = mybir.dt.bfloat16
U32 = mybir.dt.uint32
ALU = mybir.AluOpType
ACT = mybir.ActivationFunctionType
AX = mybir.AxisListType.X

P = 128
S, HID = 1024, 512
NT = S // P
GT = 4
GW = GT * P
NG = NT // GT
HC = HID // P
H, NOPE, ROPE, VD = 32, 128, 64, 128
QR, KVR = 192, 64
NP = H // 2
IH, ID, TOPK = 16, 128, 128
E, R = 8, 16
EPS = 1e-5
CKV, CPE, CIW, CRT, CLO = QR, QR + KVR, QR + KVR + ROPE, QR + KVR + ROPE + IH, QR + KVR + ROPE + IH + E
NPROJ = CLO + E * R
SCALE = float(NOPE + ROPE) ** -0.5
IW_SCALE = float(IH) ** -0.5 * float(ID) ** -0.5
LORA_SCALE = 2.0
FUTURE = -3.0e38
TAKEN = -3.4e38
BAR = -3.2e38
MASKED = -1.0e30
ROUNDS = TOPK // 8
SLOTS = 4
TOP_INDEX = {4: 2, 5: 2}
TOP_WEIGHTS = {1: 2, 2: 2, 3: 2, 6: 2}
TOP_ATTEND = {7: 1}
LATE = min(TOP_ATTEND)
SPLIT = 5
LAG = 2
WV_FIRST = 4
WV_LAST = 2
NBUF = 4
EXTRA = ({1: ("c", 0), 3: ("pe", 0), 4: ("o", 0), 5: ("o", 1)},
         {0: ("c", 0), 1: ("pe", 0), 3: ("o", 0), 5: ("o", 1)})
SWAP = [i ^ 1 for i in range(32)]


def extent(t):
    return (t + 1) * P


def acc_at(t):
    return sum(extent(k) for k in range(1, t))


def mask_at(t):
    return sum(extent(k) for k in range(t))


def splits(t):
    n = t + 1
    if n <= 4:
        return [(0, n)]
    return [(0, (n + 1) // 2), ((n + 1) // 2, n // 2)]


def plan(g):
    out = []
    for j in range(2 * GT):
        t = GT * g + j % GT
        for b0, nb in splits(t):
            out.append((j, j // GT, j % GT, t, b0, nb))
    return out


def uses(g):
    chunks = plan(g)
    out = []
    for j in range(2 * GT):
        if j in EXTRA[g]:
            out.append(EXTRA[g][j] + (j,))
        for c, ch in enumerate(chunks):
            if ch[0] == j:
                out.append(("chunk", c, j))
    return out


def rounds(per):
    ops = []
    for k in range(max(per.values())):
        now = [t for t in per if per[t] > k]
        ops += [(t, True) for t in now] + [(t, False) for t in now]
    out = []
    for n, (t, is_max) in enumerate(ops):
        before = [m for m in range(n) if ops[m] == (t, not is_max)]
        last = [m for m in range(len(ops)) if ops[m] == (t, not is_max)]
        out.append((t, is_max, (before or last)[-1], bool(before)))
    return out


def transposed(g, p, j):
    chunks = plan(g)
    q = p if j >= 0 else p - 1
    return q * len(chunks) + (1 + max(c for c, ch in enumerate(chunks) if ch[0] == j % 8))


def build(nc, A):
    with ExitStack() as ctx:
        def sb(name, shape, dt=F32):
            return ctx.enter_context(nc.sbuf_tensor(name, shape, dt))

        def psum(name, shape):
            return ctx.enter_context(nc.psum_tensor(name, shape, F32))

        def sem(name):
            return ctx.enter_context(nc.semaphore(name))

        psS = psum("psS", [P, 2, 1024])
        psT = psum("psT", [P, 2, 512])
        psO = psum("psO", [P, 2, 512])

        OT = sb("OT", [P, NP * S])
        OTv = OT[:, :].rearrange("p (n s) -> p n s", n=NP)
        Wvo = sb("Wvo", [P, (NP - WV_FIRST - WV_LAST) * HID])
        Wc1 = sb("Wc1", [P, NP * P])
        low = sb("low", [P, NP * P])
        Wc2 = low[0:QR - P, :]
        KT = sb("KT", [P, S])
        KF = sb("KF", [P, S])
        ikT = sb("ikT", [P, S])
        qh = sb("qh", [P, S], F32R)
        ql = sb("ql", [P, S], F32R)
        qr = sb("qr", [P, S], F32R)
        acc = sb("acc", [P, acc_at(NT)])
        maskb = sb("maskb", [P, mask_at(NT)], BF16)
        Vhl = sb("Vhl", [P, NT, 2, KVR], F16)
        iw = sb("iw", [P, NT, IH])
        ropeC = sb("ropeC", [P, S])
        ropeS = sb("ropeS", [P, S])
        ident = sb("ident", [P, P])
        stage = sb("stage", [P, 4, P])
        Wh = sb("Wh", [P, 4, P], F32R)
        Wl = sb("Wl", [P, 4, P], F32R)
        wslot = sb("wslot", [P, 2, HC, P])
        Sm = sb("Sm", [P, 2, S])
        Pr = sb("Pr", [P, 2, S])
        PTh = sb("PTh", [P, NBUF, 512], F16)
        PTl = sb("PTl", [P, NBUF, 512], F16)
        qAB = sb("qAB", [P, 2, GW])
        cT = ikT[:, 0:GW]
        m1 = ikT[:, GW:2 * GW]
        m2 = sb("m2", [P, GW])
        nmax = sb("nmax", [P, 2 * GT])
        den = sb("den", [P, 2 * GT])
        rden = sb("rden", [P, 2 * GT])
        osum = sb("osum", [P, 2, GT, KVR])
        On = sb("On", [P, GT, 2, KVR])
        top8 = sb("top8", [P, NT, 8])
        small = sb("small", [P, 320])
        wkv2 = sb("wkv2", [P, 1])

        def early(lo, n):
            return OT[:, lo:lo + n]

        at = 0
        xin = early(at, NT * HID).rearrange("p (t d) -> p t d", t=NT); at += NT * HID
        pj = early(at, NT * NPROJ).rearrange("p (t n) -> p t n", t=NT); at += NT * NPROJ
        xnT = early(at, HC * S).rearrange("p (c s) -> p c s", c=HC); at += HC * S
        wflat = early(at, HC * NPROJ)
        wproj = wflat.rearrange("p (c n) -> p c n", c=HC); at += HC * NPROJ
        ktab = early(at, NT * ROPE).rearrange("p (t a n) -> p t a n", t=NT, a=2); at += NT * ROPE
        wqb = early(at, QR); at += QR
        wkvb = early(at, KVR); at += KVR
        assert at <= NP * S
        WbT = early(0, HC * HID).rearrange("p (c n) -> p c n", c=HC)
        hwT = early(HC * HID, S)
        gx = early(HC * HID + S, HC * P).rearrange("p (c n) -> p c n", c=HC)
        ybuf = early(HC * HID + S + HC * P, HID)
        assert HC * HID + S + HC * P + HID <= NT * HID
        loraB = wflat[:, 0:HID]
        gh = wflat[:, HID:HID + P]
        y_dram = nc.dram_tensor("y_scratch", [NT, P, HID], F32, kind="Internal").ap()
        wvo_dram = nc.dram_tensor("wvo_scratch", [P, WV_FIRST * HID], F32, kind="Internal").ap()
        ikw = Sm[:, 0, 0:HC * ID].rearrange("p (c n) -> p c n", c=HC)
        hwsb = ropeC[:, :]
        hw = hwsb.rearrange("p (t e r) -> p t e r", t=NT, e=E)
        kbuf = Wvo[:, 0:NT * 192].rearrange("p (t n) -> p t n", t=NT)
        qn = Wvo[:, NT * 192:NT * 384].rearrange("p (t n) -> p t n", t=NT)
        latn = Wvo[:, NT * 384:NT * 448].rearrange("p (t n) -> p t n", t=NT)
        tmp = Wvo[:, NT * 448:NT * (448 + 192)].rearrange("p (t n) -> p t n", t=NT)
        ktmp = ropeS[:, 0:NT * 64].rearrange("p (t n) -> p t n", t=NT)
        hslot = [b[:, 2 * k:2 * k + 2, :].bitcast(F32).rearrange("p a n -> p (a n)") for b in (PTh, PTl) for k in range(2)]
        oslot = [Pr[:, k // 2, (k % 2) * HID:(k % 2) * HID + HID] for k in range(SLOTS)]
        bias = low[:, 0:HID]

        def wvo_of(p):
            if p < WV_FIRST:
                return (qh, ql)[p // 2][:, (p % 2) * HID:(p % 2) * HID + HID].bitcast(F32)
            if p >= NP - WV_LAST:
                return wslot[:, p - (NP - WV_LAST), :, :].rearrange("p c n -> p (c n)")
            return Wvo[:, (p - WV_FIRST) * HID:(p - WV_FIRST + 1) * HID]

        def following(g, p, last):
            if not last:
                return g, p + 1
            return (g + 1, 0) if g + 1 < NG else None

        def sems(names):
            return [sem(n) for n in names.split()]

        (s_w, s_w2, s_ident, s_mv, s_sd, s_xn, s_xt, s_xc, s_pj, s_pjc, s_ik, s_ikc, s_kq, s_kt, s_ktc,
         s_vec, s_rexp, s_sq, s_rms, s_pool, s_ktl, s_hw, s_hwt, s_hwc, s_gw, s_gcp, s_gm, s_gc, s_ysp, s_accz, s_rope, s_wvspill, s_pair, s_whi, s_wlo,
         s_wm, s_wcc, s_wvc, s_init, s_passed) = sems(
            "s_w s_w2 s_ident s_mv s_sd s_xn s_xt s_xc s_pj s_pjc s_ik s_ikc s_kq s_kt s_ktc "
            "s_vec s_rexp s_sq s_rms s_pool s_ktl s_hw s_hwt s_hwc s_gw s_gcp s_gm s_gc s_ysp s_accz s_rope s_wvspill s_pair s_whi s_wlo "
            "s_wm s_wcc s_wvc s_init s_passed")
        s_wd = [sem(f"s_wd{k}") for k in range(SLOTS)]
        s_topi, s_topw, s_topa, s_mask0, s_mask1 = sems("s_topi s_topw s_topa s_mask0 s_mask1")

        block = ctx.enter_context(nc.Block())

        def own(eng):
            eng.sem_inc(s_passed, 1)

        s_x = [sem(f"s_x{t}") for t in range(NT)]
        IX = [dict(zip("dma0 dma1 q qc sc relu acc".split(),
                       sems(" ".join(f"ix{g}_{n}" for n in "dma0 dma1 q qc sc relu acc".split()))))
              for g in range(NG)]
        AT = [dict(zip("qp qa qb sc masked exp pt cps m1 m2 rot ocp hi lo on onrm otr ot ln".split(),
                       sems(" ".join(f"at{g}_{n}" for n in
                                     "qp qa qb sc masked exp pt cps m1 m2 rot ocp hi lo on onrm otr ot ln".split()))))
              for g in range(NG)]
        (s_back, s_gy, s_ge, s_fin, s_fd0, s_fd1, s_fo0, s_fo1, s_fadd) = sems(
            "s_back s_gy s_ge s_fin s_fd0 s_fd1 s_fo0 s_fo1 s_fadd")

        def yout(t):
            return Sm[:, t % 2, HID:2 * HID]

        def load_head(sp, slot, h):
            sp.dma_start(hslot[slot][:, 0:QR + 2 * KVR],
                         A["headw"][bass.ds(h, 1)].rearrange("a p n -> p (a n)")).then_inc(s_wd[slot], 16)
            sp.dma_start(oslot[slot], A["o_w"][bass.ds(h * VD, VD), :]).then_inc(s_wd[slot], 16)

        def load_index(sp, s, slot, n):
            sp.dma_start(wslot[:, slot, :, :],
                         A["iq_w"].rearrange("(c p) n -> p c n", p=P)[:, :, bass.ds(n * ID, ID)]).then_inc(s[f"dma{slot}"], 16)

        def load_pair(sp, p):
            sp.dma_start(stage[:, 2:4, :], A["pairw"][bass.ds(p, 1)].rearrange("a b r n -> (a r) b n")).then_inc(s_pair, 16)
            sp.dma_start(stage[:, 0, :], Wc1[:, bass.ds(p * P, P)]).then_inc(s_pair, 16)
            for half in range(2):
                sp.dma_start(stage[half * KVR:(half + 1) * KVR, 1, :], Wc2[:, bass.ds(p * P, P)]).then_inc(s_pair, 16)

        @block.sync
        def _(sp):
            for t in range(NT):
                sp.dma_start(xin[:, t, :], A["x"][t * P:(t + 1) * P, :]).then_inc(s_x[t], 16)
                if t == NT // 2 - 1:
                    sp.dma_start(wproj, A["wproj"].rearrange("(c p) n -> p c n", p=P)).then_inc(s_w, 16)
            sp.dma_start(ikw, A["ik_w"].rearrange("(c p) n -> p c n", p=P)).then_inc(s_w2, 16)
            for dst, src in ((wqb, A["wq_norm"].partition_broadcast(P)), (wkvb, A["wkv_norm"].partition_broadcast(P)),
                             (ktab, A["ktab"].rearrange("(t p) a n -> p t a n", p=P)),
                             (wkv2[0:KVR, :], A["wkv_norm"].rearrange("(n a) -> n a", a=1)),
                             (wkv2[KVR:P, :], A["wkv_norm"].rearrange("(n a) -> n a", a=1))):
                sp.dma_start(dst, src).then_inc(s_w2, 16)
            for g in (1, 0):
                s = IX[g]
                if g:
                    load_index(sp, s, 0, 0)
                    load_index(sp, s, 1, 1)
                    sp.wait_ge(s_pj, NT)
                    sp.dma_start(WbT, A["WbT"].rearrange("(c p) n -> p c n", p=P)).then_inc(s_gw, 16)
                    sp.dma_start(loraB, A["lora_B"]).then_inc(s_gw, 16)
                else:
                    sp.wait_ge(IX[1]["q"], IH)
                    load_index(sp, s, 0, 0)
                    load_index(sp, s, 1, 1)
                    sp.wait_ge(s_hwc, NT)
                    sp.dma_start(ropeC[:, :], A["ropeC"]).then_inc(s_rope, 16)
                    sp.dma_start(ropeS[:, :], A["ropeS"]).then_inc(s_rope, 16)
                with sp.Fori(1, IH // 2) as i:
                    for slot in range(2):
                        sp.wait_ge(s["q"], i * 2 + (slot - 1))
                        load_index(sp, s, slot, i * 2 + slot)
            for slot in range(SLOTS):
                load_head(sp, slot, slot)
            sp.wait_ge(s_wcc, 4)
            load_pair(sp, 0)
            with sp.Fori(1, H // SLOTS) as i:
                for slot in range(SLOTS):
                    sp.wait_ge(s_wm, i * (2 * SLOTS) + (2 * slot + 2 - 2 * SLOTS))
                    load_head(sp, slot, i * SLOTS + slot)
            for g in range(NG):
                with sp.Fori(1 - g, NP) as p:
                    sp.wait_ge(s_wlo, p + g * NP)
                    load_pair(sp, p)
            sp.wait_ge(AT[1]["qp"], 2 * NP)
            for dst, src in ((qh[:, :].bitcast(F32), wvo_dram[:, 0:S]), (ql[:, :].bitcast(F32), wvo_dram[:, S:2 * S]),
                             (bias, A["b_base"].partition_broadcast(P))):
                sp.dma_start(dst, src).then_inc(s_back, 16)
            sp.wait_ge(AT[1]["exp"], NP * 2 * GT)
            sp.wait_ge(AT[1]["otr"], 2 * NP)
            sp.wait_ge(s_ysp, 16 * NT)
            for t in range(NT):
                if t >= 2:
                    sp.wait_ge(s_fadd, t - 1)
                    sp.dma_start(A["out"][(t - 2) * P:(t - 1) * P, :], yout(t)).then_inc((s_fo0, s_fo1)[t % 2], 16)
                sp.dma_start(Pr[:, t % 2, HID:2 * HID], y_dram[t]).then_inc((s_fd0, s_fd1)[t % 2], 16)
                sp.dma_start(Sm[:, t % 2, 0:HID], A["x"][t * P:(t + 1) * P, :]).then_inc((s_fd0, s_fd1)[t % 2], 16)
            for t in range(NT - 2, NT):
                sp.wait_ge(s_fadd, t + 1)
                sp.dma_start(A["out"][t * P:(t + 1) * P, :], yout(t)).then_inc((s_fo0, s_fo1)[t % 2], 16)
            sp.wait_ge(s_fo0, 16 * NT // 2)
            sp.wait_ge(s_fo1, 16 * NT // 2)

        @block.gpsimd
        def _(pool):
            nc.gpsimd.memset(ident[:, :], 0.0).then_inc(s_init, 1)
            nc.gpsimd.memset(acc[:, :], 0.0).then_inc(s_init, 1)
            nc.gpsimd.memset(maskb[:, 0:P], 0.0).then_inc(s_init, 1)
            nc.gpsimd.iota(small[:, 312:320].bitcast(mybir.dt.int32), pattern=[[1, E]], base=0, channel_multiplier=0).then_inc(s_init, 1)
            pool.wait_ge(s_init, 4)
            nc.gpsimd.affine_select(out=ident[:, :], in_=ident[:, :], compare_op=ALU.not_equal, fill=1.0,
                                    base=0, pattern=[[-1, P]], channel_multiplier=1).then_inc(s_ident, 1)
            nc.gpsimd.affine_select(out=maskb[:, 0:P], in_=maskb[:, 0:P], compare_op=ALU.is_ge, fill=MASKED,
                                    base=0, pattern=[[-1, P]], channel_multiplier=1).then_inc(s_accz, 1)
            for t in range(1, NT):
                d = acc[:, acc_at(t) + t * P:acc_at(t) + (t + 1) * P]
                nc.gpsimd.affine_select(out=d, in_=d, compare_op=ALU.is_ge, fill=FUTURE,
                                        base=0, pattern=[[-1, P]], channel_multiplier=1).then_inc(s_accz, 1)

            G = nc.gpsimd
            np_ = [0]

            def link(ins):
                np_[0] += 1
                ins.then_inc(s_pool, 1)
                pool.wait_ge(s_pool, np_[0])

            rq, rk = small[:, 64:72], small[:, 72:80]
            pool.wait_ge(s_rms, 1)
            pool.wait_ge(s_w2, 16 * 6)
            pool.wait_ge(s_pjc, NT)
            link(G.tensor_tensor(latn, pj[:, :, CKV:CKV + KVR], rk.unsqueeze(2).broadcast_to([P, NT, KVR]), ALU.mult))
            wk3 = wkvb.unsqueeze(1).broadcast_to([P, NT, KVR])
            link(G.tensor_tensor(kbuf[:, :, 0:KVR], latn, wk3, ALU.mult))
            link(G.tensor_tensor(kbuf[:, :, 128:192], latn, wk3, ALU.mult))
            link(G.tensor_copy(Vhl[:, :, 0, :], latn))
            link(G.tensor_tensor(Vhl[:, :, 1, :], latn, Vhl[:, :, 0, :], ALU.subtract))
            kp = pj[:, :, CPE:CPE + ROPE].rearrange("p t (i a) -> p t i a", a=2)
            ro = kbuf[:, :, KVR:KVR + ROPE].rearrange("p t (i a) -> p t i a", a=2)
            kt4 = ktmp.rearrange("p t (i a) -> p t i a", a=2)
            cos, sin = ktab[:, :, 0, :], ktab[:, :, 1, :]
            link(G.tensor_tensor(ro[:, :, :, 0], kp[:, :, :, 0], cos, ALU.mult))
            link(G.tensor_tensor(ro[:, :, :, 1], kp[:, :, :, 1], cos, ALU.mult))
            link(G.tensor_tensor(kt4[:, :, :, 0], kp[:, :, :, 1], sin, ALU.mult))
            link(G.tensor_tensor(kt4[:, :, :, 1], kp[:, :, :, 0], sin, ALU.mult))
            link(G.tensor_tensor(ro[:, :, :, 0], ro[:, :, :, 0], kt4[:, :, :, 0], ALU.subtract))
            link(G.tensor_tensor(ro[:, :, :, 1], ro[:, :, :, 1], kt4[:, :, :, 1], ALU.add))
            link(G.tensor_tensor(qn, pj[:, :, 0:QR], rq.unsqueeze(2).broadcast_to([P, NT, QR]), ALU.mult))
            G.tensor_tensor(qn, qn, wqb.unsqueeze(1).broadcast_to([P, NT, QR]), ALU.mult).then_inc(s_kq, 1)

            def split(n):
                pool.wait_ge(s_whi, n + 1)
                nc.gpsimd.tensor_tensor(Wl[:, :, :], stage[:, :, :], Wh[:, :, :].bitcast(F32), ALU.subtract).then_inc(s_wlo, 1)

            def before(g, s, p, left):
                if not isinstance(p, int) or p:
                    pool.wait_ge(s["sc"], p * 8 - left)
                elif g:
                    pool.wait_ge(AT[g - 1]["sc"], NP * 8 - left)

            def queries(g, s, cols, p, split_next=True):
                pool.wait_ge(s["m2"], p + 1)
                nc.gpsimd.tensor_tensor(m2[:, :], m2[:, :], ropeS[:, cols], ALU.mult).then_inc(s["rot"], 1)
                pool.wait_ge(s["cps"], p + 1)
                before(g, s, p, 4)
                own(pool)
                nc.gpsimd.tensor_copy(qAB[0:64, 0, :], cT[0:64, :]).then_inc(s["qa"], 1)
                pool.wait_ge(s["m1"], p + 1)
                pool.wait_ge(s["rot"], p + 1)
                nc.gpsimd.tensor_tensor(qAB[64:P, 0, :], m1[64:P, :], m2[64:P, :], ALU.add).then_inc(s["qa"], 1)
                if split_next:
                    pool.wait_ge(s["qa"], p * 2 + 2)
                    split(p + (g * NP + 1))
                    pool.wait_ge(s_wlo, p + (g * NP + 2))
                before(g, s, p, 0)
                own(pool)
                nc.gpsimd.tensor_copy(qAB[64:P, 1, :], cT[64:P, :]).then_inc(s["qb"], 1)
                nc.gpsimd.tensor_tensor(qAB[0:64, 1, :], m1[0:64, :], m2[0:64, :], ALU.add).then_inc(s["qb"], 1)

            def gate_tile(i, first):
                if not first:
                    pool.wait_ge(s_gm, i)
                own(pool)
                nc.gpsimd.tensor_copy(gx, xnT[:, :, bass.ds(i * P, P)]).then_inc(s_gcp, 1)
                nc.gpsimd.tensor_copy(gh, hwT[:, bass.ds(i * P, P)]).then_inc(s_gcp, 1)

            pool.wait_ge(s_hwc, NT)
            pool.wait_ge(s_pj, NT)
            gate_tile(0, True)
            split(0)
            with pool.Fori(1, NT) as i:
                gate_tile(i, False)
            pool.wait_ge(s_rope, 32)
            pool.wait_ge(IX[0]["sc"], IH * (GT - 1))
            for g in range(NG):
                s = AT[g]
                cols = slice(g * GW, (g + 1) * GW)
                queries(g, s, cols, 0)
                with pool.Fori(1, NP - g) as p:
                    queries(g, s, cols, p)
            queries(NG - 1, AT[NG - 1], slice((NG - 1) * GW, NG * GW), NP - 1, False)

        def act_index(act, g):
            s = IX[g]
            tiles = [t for t in range(GT * g, GT * g + GT) if t]
            n = len(tiles)

            def head(i, slot, first):
                act.wait_ge(s["q"], i * 2 + (slot + 1))
                if not first:
                    act.wait_ge(s["sc"], i * (2 * n) + (slot * n - n))
                nc.scalar.activation(qAB[:, slot, :], psT[:, slot, :], ACT.Copy).then_inc(s["qc"], 1)
                for k, t in enumerate(tiles):
                    idx = i * (2 * n) + (slot * n + k)
                    act.wait_ge(s["sc"], idx + 1)
                    if not (first and slot * n + k < 2):
                        act.wait_ge(s["acc"], idx - 1)
                    b = (slot * n + k) % 2
                    nc.scalar.activation(Sm[:, b, 0:extent(t)], psS[:, b, 0:extent(t)], ACT.Relu).then_inc(s["relu"], 1)

            if g == 0:
                act.wait_ge(IX[1]["acc"], IH * GT)
            head(0, 0, True)
            head(0, 1, True)
            with act.Fori(1, IH // 2) as i:
                head(i, 0, False)
                head(i, 1, False)
        @block.scalar
        def _(act):
            def deviation(h):
                act.wait_ge(s_mv, h + 1)
                nc.scalar.activation(small[:, 24 + 4 * h:28 + 4 * h], small[:, 16 + 4 * h:20 + 4 * h], ACT.Sqrt).then_inc(s_sd, 1)

            deviation(0)
            for t in range(NT + 1):
                if t == NT // 4:
                    deviation(1)
                if t < NT:
                    act.wait_ge(s_xt, t + 1)
                    nc.scalar.activation(xnT[:, :, t * P:(t + 1) * P], psT[:, t % 2, :].rearrange("p (c n) -> p c n", c=HC),
                                         ACT.Copy).then_inc(s_xc, 1)
                if t:
                    act.wait_ge(s_pj, t)
                    nc.scalar.activation(pj[:, t - 1, :], psO[:, (t - 1) % 2, 0:NPROJ], ACT.Copy).then_inc(s_pjc, 1)
            act.wait_ge(s_sq, 1)
            nc.scalar.activation(small[:, 64:80], small[:, 48:64], ACT.Sqrt).then_inc(s_sd, 1)
            for k in range(2):
                act.wait_ge(s_ik, k + 1)
                nc.scalar.activation(ikT[:, k * 512:(k + 1) * 512], psS[:, 0, k * 512:(k + 1) * 512], ACT.Copy).then_inc(s_ikc, 1)
            act.wait_ge(s_rexp, 1)
            nc.scalar.activation(small[:, 88:152], small[:, 88:152], ACT.Exp).then_inc(s_rexp, 1)
            act_index(act, 1)
            for t in range(NT):
                act.wait_ge(s_kt, t + 1)
                c = slice(t * P, (t + 1) * P)
                nc.scalar.activation(KT[:, c], psT[:, t % 2, 0:P], ACT.Copy).then_inc(s_ktc, 1)
                nc.scalar.activation(KF[:, c], psT[:, t % 2, P:2 * P], ACT.Copy).then_inc(s_ktc, 1)
                nc.scalar.activation(qh[:, c], psT[:, t % 2, 2 * P:3 * P], ACT.Copy).then_inc(s_ktc, 1)
                nc.scalar.activation(qr[0:QR - P, c], psT[0:QR - P, t % 2, 3 * P:4 * P], ACT.Copy).then_inc(s_ktc, 1)
            for t in range(NT):
                act.wait_ge(s_hwt, t + 1)
                nc.scalar.activation(hwT[:, t * P:(t + 1) * P], psO[:, t % 2, 0:P], ACT.Copy).then_inc(s_hwc, 1)
            act_index(act, 0)
            def weights_out(i, wvo):
                for k in range(SLOTS):
                    h = i * SLOTS + k
                    act.wait_ge(s_wm, i * (2 * SLOTS) + (2 * k + 1))
                    nc.scalar.activation(Wc1[:, bass.ds(h * 64, 64)], psT[:, k % 2, 0:64], ACT.Copy).then_inc(s_wcc, 1)
                    nc.scalar.activation(Wc2[:, bass.ds(h * 64, 64)], psT[0:QR - P, k % 2, 64:128], ACT.Copy).then_inc(s_wcc, 1)
                    if k % 2:
                        act.wait_ge(s_wm, i * (2 * SLOTS) + (2 * k + 2))
                        nc.scalar.activation(wvo(k // 2), psO[:, k // 2, :], ACT.Copy,
                                             scale=wkv2[:, 0:1]).then_inc(s_wvc, 1)

            def split(n):
                act.wait_ge(s_pair, n * 64 + 64)
                nc.scalar.activation(Wh[:, :, :], stage[:, :, :], ACT.Copy).then_inc(s_whi, 1)

            def gate_out(i):
                if not isinstance(i, int) or i:
                    act.wait_ge(s_ysp, i * 16)
                act.wait_ge(s_gm, i + 1)
                nc.scalar.activation(ybuf, psS[:, 1, HID:2 * HID], ACT.Copy).then_inc(s_gc, 1)
                act.wait_ge(s_gc, i + 1)
                act.dma_start(y_dram[bass.ds(i, 1)].rearrange("a p n -> (a p) n"), ybuf).then_inc(s_ysp, 16)

            def in_sm(i):
                return lambda k: Sm[:, i, k * HID:(k + 1) * HID]

            act.wait_ge(IX[0]["acc"], IH * (GT - 1))
            weights_out(0, in_sm(0))
            split(0)
            gate_out(0)
            act.wait_ge(AT[0]["qp"], 1)
            nc.scalar.activation(cT[:, :], psS[:, 0, 0:GW], ACT.Copy).then_inc(AT[0]["cps"], 1)
            weights_out(1, in_sm(1))
            gate_out(1)
            act.wait_ge(s_wvc, WV_FIRST)
            act.dma_start(wvo_dram, Sm[:, :, :].rearrange("p a n -> p (a n)")).then_inc(s_wvspill, 16)
            with act.Fori(2, H // SLOTS - 1) as i:
                weights_out(i, lambda k: Wvo[:, bass.ds(i * (2 * HID) + ((k - WV_FIRST) * HID), HID)])
                gate_out(i)
            weights_out(H // SLOTS - 1, lambda k: wslot[:, k, :, :].rearrange("p c n -> p (c n)"))
            gate_out(NT - 1)
            act.wait_ge(s_ysp, NT * 16)
            act.wait_ge(AT[0]["qp"], 2)
            split(1)
            for g in range(NG):
                s = AT[g]
                seq = uses(g)
                chunks = plan(g)
                nch = len(chunks)

                def exp(p, j, first, last_of_prev=False):
                    act.wait_ge(s["masked"], p * 8 + (j + 1))
                    if not (first and j < 2):
                        act.wait_ge(s["pt"], transposed(g, p, j - 2))
                    if not first and j % GT == 0:
                        act.wait_ge(s["onrm"], p * 2 + (j // GT - 1))
                    t = GT * g + j % GT
                    nc.scalar.activation(Pr[:, j % 2, 0:extent(t)], Sm[:, j % 2, 0:extent(t)], ACT.Exp,
                                         bias=nmax[:, j:j + 1], scale=-1.0, accum_out=den[:, j:j + 1]).then_inc(s["exp"], 1)

                def cross(p, h, first):
                    act.wait_ge(s["on"], p * nch + nch // 2 * (h + 1))
                    if not first:
                        act.wait_ge(s["onrm"], p * 2 + (h - 1))
                    o = psO[:, h, :].rearrange("p (t a n) -> p t a n", t=GT, a=2)
                    nc.scalar.activation(osum[:, h, :, :], o[:, :, 1, :], ACT.Copy).then_inc(s["ocp"], 1)

                def body(p, first, last, final=False):
                    for u, (kind, c, j) in enumerate(seq):
                        bank = u % 2
                        if kind == "chunk" and (c == 0 or chunks[c - 1][0] != j):
                            if j == SPLIT and not final:
                                gn, pn = following(g, p, last)
                                act.wait_ge(AT[gn]["qp"], pn * 2 + 2)
                                split(p + (g * NP + 2))
                            if j < 7:
                                exp(p, j + 1, first)
                            elif not last:
                                exp(p + 1, 0, False)
                        if kind == "c":
                            nxt = following(g, p, last)
                            if nxt:
                                act.wait_ge(AT[nxt[0]]["qp"], nxt[1] * 2 + 1)
                                act.wait_ge(s["qb"], p * 2 + 2)
                                nc.scalar.activation(cT[:, :], psT[:, bank, :], ACT.Copy).then_inc(AT[nxt[0]]["cps"], 1)
                        elif kind == "o" and not first:
                            act.wait_ge(s["otr"], p * 2 + (c - 1))
                            nc.scalar.activation(OT[:, bass.ds((p - 1) * S + (g * GW + c * GW // 2), GW // 2)],
                                                 psT[:, bank, 0:GW // 2], ACT.Copy).then_inc(s["ot"], 1)
                        elif kind == "chunk":
                            nb = chunks[c][5]
                            act.wait_ge(s["pt"], p * nch + (c + 1))
                            if not (first and c < NBUF):
                                act.wait_ge(s["on"], p * nch + (c - NBUF + 1))
                            nc.scalar.activation(PTh[:, c % NBUF, 0:nb * P], psT[:, bank, 0:nb * P], ACT.Copy).then_inc(s["hi"], 1)
                            done = c - LAG
                            if done == nch // 2 - 1:
                                cross(p, 0, first)
                            elif done + nch == nch - 1 and not first:
                                cross(p - 1, 1, False)

                if g:
                    act.wait_ge(AT[0]["onrm"], 2 * NP)
                exp(0, 0, True)
                body(0, True, False)
                with act.Fori(1, NP - 1 - g) as p:
                    body(p, False, False)
                if g:
                    body(NP - 2, False, False, True)
                body(NP - 1, False, True, bool(g))
                cross(NP - 1, 1, False)
                for c in range(2):
                    act.wait_ge(s["otr"], 2 * NP - 1 + c)
                    at = (NP - 1) * S + g * GW + c * GW // 2
                    nc.scalar.activation(OT[:, at:at + GW // 2], psT[:, c, 0:GW // 2], ACT.Copy).then_inc(s["ot"], 1)
            for t in range(NT):
                act.wait_ge(s_gy, t + 1)
                nc.scalar.activation(Pr[:, t % 2, 0:HID], Pr[:, t % 2, HID:2 * HID], ACT.Exp, scale=-1.0).then_inc(s_ge, 1)

        @block.vector
        def _(dve):
            nv = [0]
            V = nc.vector

            def link(ins):
                nv[0] += 1
                ins.then_inc(s_vec, 1)
                dve.wait_ge(s_vec, nv[0])

            def rsqrt_refine(out, x, y, t1):
                link(V.reciprocal(t1, y))
                link(V.tensor_tensor(out, t1, t1, ALU.mult))
                link(V.tensor_tensor(out, out, x, ALU.mult))
                link(V.tensor_scalar(out, out, -0.5, 1.5, ALU.mult, ALU.add))
                link(V.tensor_tensor(out, out, t1, ALU.mult))

            for h in range(2):
                tiles = range(h * NT // 2, (h + 1) * NT // 2)
                for t in tiles:
                    dve.wait_ge(s_x[t], 16)
                    link(V.bn_stats(small[:, 160 + 6 * t:166 + 6 * t], xin[:, t, :]))
                    link(V.bn_aggr(small[:, 2 * t:2 * t + 2], small[:, 160 + 6 * t:166 + 6 * t]))
                mv = small[:, 8 * h:8 * h + 8].rearrange("p (t a) -> p t a", a=2)
                var, sd, rs, t1 = (small[:, at + 4 * h:at + 4 * h + 4] for at in (16, 24, 32, 40))
                V.tensor_scalar(var, mv[:, :, 1], EPS, None, ALU.add).then_inc(s_mv, 1)
                dve.wait_ge(s_sd, h + 1)
                dve.wait_ge(s_mv, h + 1)
                rsqrt_refine(rs, var, sd, t1)
                for t in tiles:
                    V.tensor_scalar(xin[:, t, :], xin[:, t, :], small[:, 2 * t:2 * t + 1], small[:, 32 + t:33 + t],
                                    ALU.subtract, ALU.mult).then_inc(s_xn, 1)
            dve.wait_ge(s_pjc, NT)
            link(V.tensor_tensor(tmp, pj[:, :, 0:QR], pj[:, :, 0:QR], ALU.mult))
            link(V.tensor_reduce(small[:, 48:56], tmp, AX, ALU.add))
            link(V.tensor_tensor(tmp[:, :, 0:KVR], pj[:, :, CKV:CKV + KVR], pj[:, :, CKV:CKV + KVR], ALU.mult))
            link(V.tensor_reduce(small[:, 56:64], tmp[:, :, 0:KVR], AX, ALU.add))
            link(V.tensor_scalar(small[:, 48:56], small[:, 48:56], 1.0 / QR, EPS, ALU.mult, ALU.add))
            V.tensor_scalar(small[:, 56:64], small[:, 56:64], 1.0 / KVR, EPS, ALU.mult, ALU.add).then_inc(s_sq, 1)
            lg = pj[:, :, CRT:CRT + E]
            ex = small[:, 88:152].rearrange("p (t e) -> p t e", t=NT)
            link(V.tensor_reduce(small[:, 80:88], lg, AX, ALU.max))
            V.tensor_tensor(ex, lg, small[:, 80:88].unsqueeze(2).broadcast_to([P, NT, E]), ALU.subtract).then_inc(s_rexp, 1)
            link(V.tensor_scalar(iw[:, :, :], pj[:, :, CIW:CIW + IH], IW_SCALE, None, ALU.mult))
            dve.wait_ge(s_sd, 3)
            dve.wait_ge(s_sq, 1)
            rsqrt_refine(small[:, 64:80], small[:, 48:64], small[:, 64:80], small[:, 288:304])
            dve.sem_inc(s_rms, 1)
            dve.wait_ge(s_rexp, 2)
            link(V.tensor_reduce(small[:, 304:312], ex, AX, ALU.add))
            link(V.reciprocal(small[:, 304:312], small[:, 304:312]))
            link(V.tensor_tensor(ex, ex, small[:, 304:312].unsqueeze(2).broadcast_to([P, NT, E]), ALU.mult))
            t8 = tmp[:, 0:NT, 64:72]
            i8 = tmp[:, 0:NT, 72:80].bitcast(U32)
            f8 = tmp[:, 0:NT, 80:88]
            for t in range(NT):
                link(V.max(t8[:, t, :], ex[:, t, :]))
                link(V.max_index(i8[:, t, :], t8[:, t, :], ex[:, t, :]))
            link(V.tensor_copy(f8, i8))
            dve.wait_ge(s_init, 4)
            link(V.tensor_copy(small[:, 40:48], small[:, 312:320].bitcast(mybir.dt.int32)))
            it = small[:, 40:48].unsqueeze(1).broadcast_to([P, NT, E])
            sm12 = small[:, 304:312]
            link(V.tensor_tensor(sm12, t8[:, :, 0], t8[:, :, 1], ALU.add))
            link(V.reciprocal(sm12, sm12))
            link(V.tensor_scalar(sm12, sm12, LORA_SCALE, None, ALU.mult))
            link(V.tensor_tensor(t8[:, :, 0:2], t8[:, :, 0:2], sm12.unsqueeze(2).broadcast_to([P, NT, 2]), ALU.mult))
            we = tmp[:, :, 96:104]
            w1 = tmp[:, :, 104:112]
            link(V.tensor_tensor(we, it, f8[:, :, 0:1].broadcast_to([P, NT, E]), ALU.is_equal))
            link(V.tensor_tensor(we, we, t8[:, :, 0:1].broadcast_to([P, NT, E]), ALU.mult))
            link(V.tensor_tensor(w1, it, f8[:, :, 1:2].broadcast_to([P, NT, E]), ALU.is_equal))
            link(V.tensor_tensor(w1, w1, t8[:, :, 1:2].broadcast_to([P, NT, E]), ALU.mult))
            link(V.tensor_tensor(we, we, w1, ALU.add))
            V.tensor_tensor(hw, pj[:, :, CLO:CLO + E * R].rearrange("p t (e r) -> p t e r", e=E),
                            we.unsqueeze(3).broadcast_to([P, NT, E, R]), ALU.mult).then_inc(s_hw, 1)
            def top(s_top, per, it, op, first):
                ops = rounds(per)
                t, is_max, before, here = ops[op]
                if here or not first:
                    dve.wait_ge(s_top, (it if here else it - 1) * len(ops) + (before + 1))
                    if not isinstance(it, int):
                        own(dve)
                a = acc[:, acc_at(t):acc_at(t) + extent(t)]
                ins = V.max(top8[:, t, :], a) if is_max else V.match_replace(a, top8[:, t, :], a, TAKEN)
                ins.then_inc(s_top, 1)

            def masks(s_mask, tiles):
                for t in tiles:
                    V.tensor_scalar(maskb[:, mask_at(t):mask_at(t) + extent(t)], acc[:, acc_at(t):acc_at(t) + extent(t)],
                                    BAR, MASKED, ALU.is_ge, ALU.mult).then_inc(s_mask, 1)

            dve.wait_ge(s_accz, NT)
            for g in (1, 0):
                s = IX[g]
                tiles = [t for t in range(GT * g, GT * g + GT) if t]
                n = len(tiles)

                def accumulate(i, slot, first):
                    head = i * 2 + slot
                    for k, t in enumerate(tiles):
                        idx = i * (2 * n) + (slot * n + k)
                        dve.wait_ge(s["relu"], idx + 1)
                        if not (first and slot == 0):
                            dve.wait_ge(s["acc"], idx - n + 1)
                        a = acc[:, acc_at(t):acc_at(t) + extent(t)]
                        sc = iw[:, t, head:head + 1] if isinstance(head, int) else iw[:, t, bass.ds(head, 1)]
                        V.scalar_tensor_tensor(a, Sm[:, (slot * n + k) % 2, 0:extent(t)], sc, a, ALU.mult, ALU.add).then_inc(s["acc"], 1)
                    if g == 0:
                        half = len(rounds(TOP_INDEX)) // 2
                        for op in range(half * slot, half * slot + half):
                            top(s_topi, TOP_INDEX, i, op, first)

                if g == 0:
                    dve.wait_ge(IX[1]["acc"], IH * GT)
                    for t in range(NT):
                        c = slice(t * P, (t + 1) * P)
                        dve.wait_ge(s_ktc, 4 * (t + 1))
                        V.tensor_tensor(ql[:, c], psT[:, t % 2, 2 * P:3 * P], qh[:, c].bitcast(F32), ALU.subtract).then_inc(s_ktl, 1)
                        V.tensor_tensor(qr[QR - P:P, c], psT[0:QR - P, t % 2, 3 * P:4 * P], qr[0:QR - P, c].bitcast(F32),
                                        ALU.subtract).then_inc(s_ktl, 1)
                accumulate(0, 0, True)
                accumulate(0, 1, True)
                with dve.Fori(1, IH // 2) as i:
                    accumulate(i, 0, False)
                    accumulate(i, 1, False)
            def rope(g, pe_out):
                own(dve)
                V.stream_shuffle(m2[:, :], pe_out, SWAP).then_inc(AT[g]["m2"], 1)
                V.tensor_tensor(m1[:, :], pe_out, ropeC[:, g * GW:(g + 1) * GW], ALU.mult).then_inc(AT[g]["m1"], 1)

            n = len(rounds(TOP_WEIGHTS))
            dve.wait_ge(IX[0]["acc"], IH * (GT - 1))
            dve.wait_ge(s_topi, len(rounds(TOP_INDEX)) * (IH // 2))
            for op in range(n):
                top(s_topw, TOP_WEIGHTS, 0, op, True)
            dve.wait_ge(s_rope, 32)
            dve.wait_ge(AT[0]["qp"], 2)
            rope(0, psS[:, 1, 0:GW])
            with dve.Fori(1, ROUNDS // 2) as i:
                for op in range(n):
                    top(s_topw, TOP_WEIGHTS, i, op, False)
            dve.wait_ge(s_topw, n * (ROUNDS // 2))
            masks(s_mask0, range(1, LATE))
            dve.wait_ge(s_mask0, LATE - 1)

            for g in range(NG):
                s = AT[g]
                seq = uses(g)
                chunks = plan(g)
                nch = len(chunks)

                def masked(p, j, first):
                    t = GT * g + j % GT
                    n = extent(t)
                    dve.wait_ge(s["sc"], p * 8 + (j + 1))
                    if not (first and j < 2):
                        dve.wait_ge(s["exp"], p * 8 + (j - 1))
                    own(dve)
                    V.tensor_tensor_reduce(Sm[:, j % 2, 0:n], psS[:, j % 2, 0:n], maskb[:, mask_at(t):mask_at(t) + n],
                                           -SCALE, 3.0e38, ALU.add, ALU.min, nmax[:, j:j + 1]).then_inc(s["masked"], 1)

                def norm(p, h, first):
                    dve.wait_ge(s["on"], p * nch + nch // 2 * (h + 1))
                    o = psO[:, h, :].rearrange("p (t a n) -> p t a n", t=GT, a=2)
                    V.reciprocal(rden[:, GT * h:GT * h + GT], den[:, GT * h:GT * h + GT]).then_inc(s["ln"], 1)
                    dve.wait_ge(s["ocp"], p * 2 + (h + 1))
                    V.tensor_tensor(osum[:, h, :, :], o[:, :, 0, :], osum[:, h, :, :], ALU.add).then_inc(s["ln"], 1)
                    dve.wait_ge(s["ln"], p * 4 + (2 * h + 2))
                    if not first and h == 0:
                        dve.wait_ge(s["otr"], p * 2)
                    V.tensor_tensor(On[:, :, h, :], osum[:, h, :, :],
                                    rden[:, GT * h:GT * h + GT].unsqueeze(2).broadcast_to([P, GT, KVR]),
                                    ALU.mult).then_inc(s["onrm"], 1)

                def body(p, first, last):
                    for u, (kind, c, j) in enumerate(seq):
                        bank = u % 2
                        if kind == "chunk" and (c == 0 or chunks[c - 1][0] != j):
                            if j < 6:
                                masked(p, j + 2, first)
                            elif not last:
                                masked(p + 1, j - 6, False)
                        if kind == "pe":
                            nxt = following(g, p, last)
                            if nxt:
                                dve.wait_ge(AT[nxt[0]]["qp"], nxt[1] * 2 + 2)
                                dve.wait_ge(s["qb"], p * 2 + 2)
                                rope(nxt[0], psT[:, bank, :])
                        elif kind == "chunk":
                            nb = chunks[c][5]
                            dve.wait_ge(s["hi"], p * nch + (c + 1))
                            V.tensor_tensor(PTl[:, c % NBUF, 0:nb * P], psT[:, bank, 0:nb * P], PTh[:, c % NBUF, 0:nb * P],
                                            ALU.subtract).then_inc(s["lo"], 1)
                            done = c - LAG
                            if done == nch // 2 - 1:
                                norm(p, 0, first)
                            elif done + nch == nch - 1 and not first:
                                norm(p - 1, 1, False)
                            every = 2 * GT // len(rounds(TOP_ATTEND))
                            if g == 0 and j % every == 0 and (c == 0 or chunks[c - 1][0] != j):
                                top(s_topa, TOP_ATTEND, p, j // every, first)

                if g:
                    dve.wait_ge(s_topa, len(rounds(TOP_ATTEND)) * ROUNDS)
                    masks(s_mask1, range(LATE, NT))
                    dve.wait_ge(s_mask1, NT - LATE)
                else:
                    dve.wait_ge(s_wvspill, 16)
                masked(0, 0, True)
                masked(0, 1, True)
                body(0, True, False)
                with dve.Fori(1, NP - 1) as p:
                    body(p, False, False)
                body(NP - 1, False, True)
                norm(NP - 1, 1, False)

            dve.wait_ge(s_back, 16 * 3)
            for t in range(NT + 1):
                if t < NT:
                    if t >= 2:
                        dve.wait_ge(s_ge, t - 1)
                    dve.wait_ge((s_fd0, s_fd1)[t % 2], 32 * (t // 2 + 1))
                    y = Pr[:, t % 2, HID:2 * HID]
                    V.tensor_tensor(y, y, bias, ALU.add).then_inc(s_gy, 1)
                if t:
                    u = t - 1
                    e, y = Pr[:, u % 2, 0:HID], Pr[:, u % 2, HID:2 * HID]
                    dve.wait_ge(s_ge, u + 1)
                    link(V.tensor_scalar(e, e, 1.0, None, ALU.add))
                    link(V.reciprocal(e, e))
                    link(V.tensor_tensor(e, e, y, ALU.mult))
                    dve.wait_ge(s_fin, u + 1)
                    if u >= 2:
                        dve.wait_ge((s_fo0, s_fo1)[u % 2], 16 * (u // 2))
                    link(V.tensor_tensor(yout(u), psO[:, u % 2, :], e, ALU.mult))
                    V.tensor_tensor(yout(u), yout(u), Sm[:, u % 2, 0:HID], ALU.add).then_inc(s_fadd, 1)

        @block.tensor
        def _(pe):
            T = nc.tensor

            def bank_read(g, s, seq, nch, p, u, first, last):
                v = u - 2
                nxt = following(g, p, last)
                while v >= 0 and (seq[v][0] in ("c", "pe") and not nxt or seq[v][0] == "o" and first):
                    v -= 2
                if v < 0 and first:
                    return
                kind, c, _ = seq[v % len(seq)]
                q = p if v >= 0 else p - 1
                if kind == "c":
                    pe.wait_ge(AT[nxt[0]]["cps"], nxt[1] + 1)
                elif kind == "pe":
                    pe.wait_ge(AT[nxt[0]]["m1"], nxt[1] + 1)
                elif kind == "o":
                    pe.wait_ge(s["ot"], q * 2 + (c - 1))
                else:
                    pe.wait_ge(s["lo"], q * nch + (c + 1))

            def mm(out, lhsT, rhs, start=True, stop=True):
                return T.matmul(out, lhsT, rhs, start=start, stop=stop)

            pe.wait_ge(s_ident, 1)
            pe.wait_ge(s_w, 16)
            for t in range(NT + 1):
                if t < NT:
                    pe.wait_ge(s_xn, t + 1)
                    if t >= 2:
                        pe.wait_ge(s_xc, t - 1)
                    for c in range(HC):
                        last = T.transpose(psT[:, t % 2, c * P:(c + 1) * P], xin[:, t, c * P:(c + 1) * P], ident[:, :])
                    last.then_inc(s_xt, 1)
                if t:
                    u = t - 1
                    pe.wait_ge(s_xc, u + 1)
                    if u >= 2:
                        pe.wait_ge(s_pjc, u - 1)
                    for c in range(HC):
                        last = mm(psO[:, u % 2, 0:NPROJ], xnT[:, c, u * P:(u + 1) * P], wproj[:, c, :], c == 0, c == HC - 1)
                    last.then_inc(s_pj, 1)
            pe.wait_ge(s_w2, 16 * 6)
            for k in range(2):
                for c in range(HC):
                    last = mm(psS[:, 0, k * 512:(k + 1) * 512], ikw[:, c, :], xnT[:, c, k * 512:(k + 1) * 512], c == 0, c == HC - 1)
                last.then_inc(s_ik, 1)
            def keys_and_latents():
                pe.wait_ge(s_kq, 1)
                pe.wait_ge(IX[1]["qc"], IH)
                for t in range(NT):
                    if t >= 2:
                        pe.wait_ge(s_ktc, 4 * (t - 1))
                        pe.wait_ge(s_ktl, 2 * (t - 1))
                    T.transpose(psT[:, t % 2, 0:P], kbuf[:, t, 0:128], ident[:, :])
                    T.transpose(psT[:, t % 2, P:2 * P], kbuf[:, t, 64:192], ident[:, :])
                    T.transpose(psT[:, t % 2, 2 * P:3 * P], qn[:, t, 0:P], ident[:, :])
                    T.transpose(psT[0:QR - P, t % 2, 3 * P:4 * P], qn[:, t, P:QR], ident[:, :]).then_inc(s_kt, 1)
                pe.wait_ge(s_hw, 1)
                for t in range(NT):
                    if t >= 2:
                        pe.wait_ge(s_hwc, t - 1)
                    T.transpose(psO[:, t % 2, 0:P], hwsb[:, t * P:(t + 1) * P], ident[:, :]).then_inc(s_hwt, 1)
                pe.wait_ge(s_ktc, 4 * NT)
                pe.wait_ge(s_ktl, 2 * NT)

            for g in (1, 0):
                if g == 0:
                    keys_and_latents()
                s = IX[g]
                tiles = [t for t in range(GT * g, GT * g + GT) if t]
                n = len(tiles)

                def project(i, slot, first):
                    pe.wait_ge(s[f"dma{slot}"], i * 16 + 16)
                    if not first:
                        pe.wait_ge(s["qc"], i * 2 + (slot - 1))
                    for c in range(HC):
                        last = mm(psT[:, slot, :], wslot[:, slot, c, :], xnT[:, c, g * GW:(g + 1) * GW], c == 0, c == HC - 1)
                    last.then_inc(s["q"], 1)

                def score(i, slot, first):
                    pe.wait_ge(s["qc"], i * 2 + (slot + 1))
                    for k, t in enumerate(tiles):
                        idx = i * (2 * n) + (slot * n + k)
                        b = (slot * n + k) % 2
                        if not (first and slot * n + k < 2):
                            pe.wait_ge(s["relu"], idx - 1)
                        q = qAB[:, slot, (t % GT) * P:(t % GT + 1) * P]
                        for lo in range(0, extent(t), 512):
                            hi = min(lo + 512, extent(t))
                            last = mm(psS[:, b, lo:hi], q, ikT[:, lo:hi])
                        last.then_inc(s["sc"], 1)

                if g == 0:
                    pe.wait_ge(IX[1]["relu"], IH * GT)
                project(0, 0, True)
                project(0, 1, True)
                score(0, 0, True)
                with pe.Fori(1, IH // 2) as i:
                    project(i, 0, False)
                    score(i - 1, 1, False)
                    project(i, 1, False)
                    score(i, 0, False)
                score(IH // 2 - 1, 1, False)
            pe.wait_ge(IX[0]["relu"], IH * (GT - 1))

            def head_weights(i, k, first):
                dst = hslot[k]
                pe.wait_ge(s_wd[k], i * 32 + 32)
                if not (first and k < 2):
                    pe.wait_ge(s_wcc, i * (2 * SLOTS) + (2 * k - 2))
                wk, wv = dst[:, QR:QR + KVR], dst[:, QR + KVR:QR + 2 * KVR]
                mm(psT[:, k % 2, 0:64], dst[:, 0:P], wk)
                mm(psT[0:QR - P, k % 2, 64:128], dst[:, P:QR], wk).then_inc(s_wm, 1)
                if not first and k % 2 == 0:
                    pe.wait_ge(s_wvc, i * 2 + (k // 2 - 1))
                mm(psO[64 * (k % 2):64 * (k % 2) + 64, k // 2, :], wv, oslot[k]).then_inc(s_wm, 1)

            def queries(g, out, part):
                cols = slice(g * GW, (g + 1) * GW)
                a, b, half = 2 * part, 2 * part + 1, QR - P
                mm(out, Wh[:, a, :], qh[:, cols], True, False)
                mm(out, Wl[:, a, :], qh[:, cols], False, False)
                mm(out, Wh[:, a, :], ql[:, cols], False, False)
                mm(out, Wh[:, b, :], qr[:, cols], False, False)
                mm(out, Wl[0:half, b, :], qr[0:half, cols], False, True).then_inc(AT[g]["qp"], 1)

            def four_heads(i, first):
                out = psS[:, 1, HID:2 * HID]
                head_weights(i, 0, first)
                head_weights(i, 1, first)
                pe.wait_ge(s_gcp, i * 2 + 2)
                if not first:
                    pe.wait_ge(s_gc, i)
                mm(out, gx[:, 0, :], WbT[:, 0, :], True, False)
                mm(out, gx[:, 1, :], WbT[:, 1, :], False, False)
                head_weights(i, 2, first)
                mm(out, gx[:, 2, :], WbT[:, 2, :], False, False)
                head_weights(i, 3, first)
                mm(out, gx[:, 3, :], WbT[:, 3, :], False, False)
                mm(out, gh, loraB, False, True).then_inc(s_gm, 1)

            pe.wait_ge(s_gw, 32)
            four_heads(0, True)
            pe.wait_ge(s_wlo, 1)
            queries(0, psS[:, 0, 0:GW], 0)
            queries(0, psS[:, 1, 0:GW], 1)
            with pe.Fori(1, H // SLOTS) as i:
                four_heads(i, False)
            pe.wait_ge(s_wcc, 2 * H)
            pe.wait_ge(s_wvc, NP)
            pe.wait_ge(s_gc, NT)
            for g in range(NG):
                s = AT[g]
                seq = uses(g)
                chunks = plan(g)
                nch = len(chunks)

                def score(p, j, first):
                    h, t = j // GT, GT * g + j % GT
                    if j == 0:
                        pe.wait_ge(s["qa"], p * 2 + 2)
                    if j == GT:
                        pe.wait_ge(s["qb"], p * 2 + 2)
                    if not (first and j < 2):
                        pe.wait_ge(s["masked"], p * 8 + (j - 1))
                    keys = KF if h else KT
                    q = qAB[:, h, (j % GT) * P:(j % GT + 1) * P]
                    for lo in range(0, extent(t), 512):
                        hi = min(lo + 512, extent(t))
                        last = mm(psS[:, j % 2, lo:hi], q, keys[:, lo:hi])
                    last.then_inc(s["sc"], 1)

                def latent(p, c, first):
                    _, h, slot, t, b0, nb = chunks[c]
                    pe.wait_ge(s["lo"], p * nch + (c + 1))
                    if c in (0, nch // 2) and not first:
                        pe.wait_ge(s["onrm"], p * 2 + (h - 1))
                    o = psO[:, h, slot * P:(slot + 1) * P]
                    for k in range(nb):
                        b = b0 + k
                        T.matmul(o, PTh[:, c % NBUF, k * P:(k + 1) * P], Vhl[:, b, :, :].rearrange("p a n -> p (a n)"),
                                 start=(b == 0), stop=(b == t))
                        last = T.matmul(o[:, 0:KVR], PTl[:, c % NBUF, k * P:(k + 1) * P], Vhl[:, b, 0, :],
                                        start=False, stop=False, skip_group_check=True)
                    last.then_inc(s["on"], 1)

                def body(p, first, last):
                    for u, (kind, c, j) in enumerate(seq):
                        bank = u % 2
                        if kind == "chunk" and (c == 0 or chunks[c - 1][0] != j):
                            if j < 6:
                                score(p, j + 2, first)
                            elif not last:
                                score(p + 1, j - 6, False)
                        nxt = following(g, p, last)
                        if kind in ("c", "pe") and not nxt or kind == "o" and first:
                            continue
                        bank_read(g, s, seq, nch, p, u, first, last)
                        if kind in ("c", "pe"):
                            if kind == "c":
                                pe.wait_ge(s_wlo, p + (g * NP + 2))
                            queries(nxt[0], psT[:, bank, :], ("c", "pe").index(kind))
                        elif kind == "o":
                            outputs(bank, p - 1, c).then_inc(s["otr"], 1)
                        else:
                            _, _, _, _, b0, nb = chunks[c]
                            if c == 0 or chunks[c - 1][0] != j:
                                pe.wait_ge(s["exp"], p * 8 + (j + 1))
                            for k in range(nb):
                                m = T.transpose(psT[:, bank, k * P:(k + 1) * P],
                                                Pr[:, j % 2, (b0 + k) * P:(b0 + k + 1) * P], ident[:, :])
                            m.then_inc(s["pt"], 1)
                            if c >= LAG:
                                latent(p, c - LAG, first)
                            elif not first:
                                latent(p - 1, nch + c - LAG, False)

                def outputs(bank, p, half):
                    pe.wait_ge(s["onrm"], p * 2 + 2)
                    for k in range(GT // 2):
                        m = T.transpose(psT[:, bank, k * P:(k + 1) * P], On[:, half * GT // 2 + k, :, :].rearrange("p a n -> p (a n)"), ident[:, :])
                    return m

                if g:
                    pe.wait_ge(AT[0]["ot"], 2 * NP)
                else:
                    pe.wait_ge(s["cps"], 1)
                    pe.wait_ge(s["m1"], 1)
                score(0, 0, True)
                score(0, 1, True)
                body(0, True, False)
                with pe.Fori(1, NP - 1) as p:
                    body(p, False, False)
                body(NP - 1, False, True)
                for c in range(nch - LAG, nch):
                    latent(NP - 1, c, False)
                pe.wait_ge(s["lo"], NP * nch)
                for half in range(2):
                    outputs(half, NP - 1, half).then_inc(s["otr"], 1)
            pe.wait_ge(AT[1]["ot"], 2 * NP)
            pe.wait_ge(s_back, 16 * 3)
            for t in range(NT):
                if t >= 2:
                    pe.wait_ge(s_fadd, t - 1)
                for p in range(NP):
                    last = mm(psO[:, t % 2, :], OTv[:, p, t * P:(t + 1) * P], wvo_of(p), p == 0, p == NP - 1)
                last.then_inc(s_fin, 1)


def kernel(**inputs):
    import numpy as np
    import concourse.bacc as bacc
    from concourse.bass_utils import run_bass_kernel_spmd as run

    f = {k.replace("L0_", ""): np.asarray(v) for k, v in inputs.items()}
    x = f["attn_hidden_states"].reshape(S, HID)
    qb = f["attn_q_b_w"].reshape(QR, H, NOPE + ROPE)
    kvb = f["attn_kv_b_w"].reshape(KVR, H, NOPE + VD)
    headw = np.concatenate([qb[:, :, :NOPE].transpose(1, 2, 0), kvb[:, :, :NOPE].transpose(1, 2, 0),
                            kvb[:, :, NOPE:].transpose(1, 2, 0)], axis=2)
    qpe = qb[:, :, NOPE:].reshape(QR, NP, 2, ROPE)[:, :, ::-1]
    pairw = qpe.reshape(QR, NP, P).transpose(1, 0, 2)
    pairw = np.stack([pairw[:, :P], np.concatenate([pairw[:, P:], pairw[:, P:]], axis=1)], axis=1)
    inv = (np.float32(1.0) / np.float32(10000.0) ** (np.arange(0, ROPE, 2, dtype=np.float32) / np.float32(ROPE))).astype(np.float32)
    ang = np.arange(S, dtype=np.float32)[:, None] * inv[None, :]
    cos, sin = np.cos(ang).astype(np.float32), np.sin(ang).astype(np.float32)
    ropeC = np.tile(np.repeat(cos.T, 2, axis=0), (2, 1))
    ropeS = np.tile(np.stack([-sin.T, sin.T], axis=1).reshape(ROPE, S), (2, 1))
    arrays = {
        "x": x,
        "wproj": np.concatenate([f["attn_q_a_w"], f["attn_kv_a_w"], f["attn_idx_weights_w"], f["ffn_W_router"].T,
                                 f["ffn_lora_A"].reshape(E * R, HID).T], axis=1),
        "ik_w": f["attn_idx_wk_w"], "iq_w": f["attn_idx_wq_w"],
        "wq_norm": f["attn_q_a_norm_w"], "wkv_norm": f["attn_kv_a_norm_w"],
        "ktab": np.stack([cos, sin], axis=1), "ropeC": ropeC, "ropeS": ropeS,
        "b_base": f["ffn_b_base"], "lora_B": f["ffn_lora_B"].transpose(0, 2, 1).reshape(E * R, HID),
        "WbT": f["ffn_W_base"].T, "headw": headw, "o_w": f["attn_o_w"], "pairw": pairw,
    }
    nc = bacc.Bacc("TRN2", target_bir_lowering=False, num_devices=1)
    named, aps = {}, {}
    for name, a in arrays.items():
        a = np.ascontiguousarray(a)
        named[f"in_{name}"] = a
        aps[name] = nc.dram_tensor(f"in_{name}", a.shape, mybir.dt.from_np(a.dtype), kind="ExternalInput").ap()
    aps["out"] = nc.dram_tensor("out_0", (S, HID), F32, kind="ExternalOutput").ap()
    build(nc, aps)
    r = run(nc, [named], core_ids=[0])
    return r.results[0]["out_0"].reshape(1, S, HID)
```
